# Optimizing a Trainium2 kernel written in Bass

```python
import numpy as np
import jax
import jax.numpy as jnp

def _softmax(x, axis=-1):
    return jax.nn.softmax(x, axis=axis)

def _gelu(x):
    return jax.nn.gelu(x, approximate=True)

def _silu(x):
    return jax.nn.silu(x)

def _sigmoid(x):
    return jax.nn.sigmoid(x)

def _layernorm(x, axis=-1, eps=1e-05):
    m = jnp.mean(x, axis=axis, keepdims=True)
    v = jnp.var(x, axis=axis, keepdims=True)
    return (x - m) / jnp.sqrt(v + eps)

def _scatter_add(tgt, idx, src, axis=0):
    return tgt.at[idx].add(src)

def _segment_sum(src, seg, n):
    return jax.ops.segment_sum(src, seg, n)
kernel_name = 'mk_sandwich_d1_jaxref_r8_1c8e9f'

def setup_inputs(seed: int=0):
    np.random.seed(seed)
    _w = jnp.asarray

    def _L0_attn_setup():
        import jax, jax.numpy as jnp
        import numpy as np
        import math
        D_MODEL = 256
        N_HEADS = 16
        D_HEAD = 128
        BATCH = 2
        SEQ = 256
        key = jax.random.key(seed)
        ks = jax.random.split(key, 5)
        std = 0.02
        x = jax.random.normal(ks[0], (BATCH, SEQ, D_MODEL), dtype=jnp.float32)
        W_Q = std * jax.random.normal(ks[1], (N_HEADS, D_HEAD, D_MODEL), dtype=jnp.float32)
        W_K = std * jax.random.normal(ks[2], (N_HEADS, D_HEAD, D_MODEL), dtype=jnp.float32)
        W_V = std * jax.random.normal(ks[3], (N_HEADS, D_HEAD, D_MODEL), dtype=jnp.float32)
        W_O = std * jax.random.normal(ks[4], (N_HEADS, D_MODEL, D_HEAD), dtype=jnp.float32)
        return {'x': x, 'W_Q': W_Q, 'W_K': W_K, 'W_V': W_V, 'W_O': W_O}
    _L0_attn_in = _L0_attn_setup()

    def _L0_ffn_setup():
        import jax, jax.numpy as jnp
        import numpy as np
        TOP_K = 8
        key = jax.random.key(seed)
        k1, k2, k3 = jax.random.split(key, 3)
        B, S, H, E = (4, 512, 256, 64)
        hidden_states = jax.random.normal(k1, (B, S, H), dtype=jnp.float32)
        router_weight = jax.random.normal(k2, (E, H), dtype=jnp.float32)
        router_bias = jnp.zeros((E,), dtype=jnp.float32)
        expert_bias = jax.random.normal(k3, (E, H), dtype=jnp.float32) * 0.1
        return {'hidden_states': hidden_states, 'router_weight': router_weight, 'router_bias': router_bias, 'expert_bias': expert_bias}
    _L0_ffn_in = _L0_ffn_setup()
    _d = {'L0_attn_x': _L0_attn_in['x'], 'L0_attn_W_Q': _L0_attn_in['W_Q'], 'L0_attn_W_K': _L0_attn_in['W_K'], 'L0_attn_W_V': _L0_attn_in['W_V'], 'L0_attn_W_O': _L0_attn_in['W_O'], 'L0_ffn_router_weight': _L0_ffn_in['router_weight'], 'L0_ffn_router_bias': _L0_ffn_in['router_bias'], 'L0_ffn_expert_bias': _L0_ffn_in['expert_bias']}
    _x0 = _d['L0_attn_x']
    _d['L0_attn_x'] = jax.random.normal(jax.random.fold_in(jax.random.key(seed), 1), (4, 256, 256), dtype=_x0.dtype)
    del _x0
    return _d

def reference(L0_attn_x, L0_attn_W_Q, L0_attn_W_K, L0_attn_W_V, L0_attn_W_O, L0_ffn_router_weight, L0_ffn_router_bias, L0_ffn_expert_bias):

    def _L0_attn_ref(x, W_Q, W_K, W_V, W_O):
        import jax, jax.numpy as jnp
        import numpy as np
        import math
        D_MODEL = 256
        N_HEADS = 16
        D_HEAD = 128
        BATCH = 2
        SEQ = 256
        d_head = W_Q.shape[1]
        seq_len = x.shape[1]
        scale = 1.0 / math.sqrt(d_head)
        q = jnp.einsum('bsd,hed->bhse', x, W_Q)
        k = jnp.einsum('bsd,hed->bhse', x, W_K)
        v = jnp.einsum('bsd,hed->bhse', x, W_V)
        scores = jnp.einsum('bhse,bhme->bhsm', q, k) * scale
        causal = jnp.triu(jnp.ones((seq_len, seq_len), dtype=bool), k=1)
        scores = jnp.where(causal, jnp.float32(-1000000000.0), scores)
        pattern = jax.nn.softmax(scores, axis=-1)
        z = jnp.einsum('bhsm,bhme->bhse', pattern, v)
        out = jnp.einsum('bhse,hde->bsd', z, W_O)
        return out

    def _L0_ffn_ref(hidden_states, router_weight, router_bias, expert_bias):
        import jax, jax.numpy as jnp
        import numpy as np
        TOP_K = 8
        B, S, H = hidden_states.shape
        flat = hidden_states.reshape(B * S, H)
        logits = jnp.einsum('th,eh->te', flat, router_weight) + router_bias
        scores = jax.nn.softmax(logits, axis=-1)
        topk_w, topk_idx = jax.lax.top_k(scores, TOP_K)
        gathered_bias = expert_bias[topk_idx]
        out = flat * jnp.sum(topk_w, axis=-1, keepdims=True) + jnp.einsum('tk,tkh->th', topk_w, gathered_bias)
        return out.reshape(B, S, H)
    x = L0_attn_x
    x = x + _layernorm(_L0_attn_ref(_layernorm(x, axis=-1), L0_attn_W_Q, L0_attn_W_K, L0_attn_W_V, L0_attn_W_O), axis=-1)
    x = x + _layernorm(_L0_ffn_ref(_layernorm(x, axis=-1), L0_ffn_router_weight, L0_ffn_router_bias, L0_ffn_expert_bias), axis=-1)
    return x

_drawn_inputs = setup_inputs


def setup_inputs(seed=0):
    import zlib

    import numpy as np

    out = dict(_drawn_inputs(seed))
    spreads = {'L0_ffn_router_bias': (0.0, 0.1)}
    factors = {}
    for name, (base, spread) in spreads.items():
        noise = np.random.default_rng([zlib.crc32(name.encode()), seed]).standard_normal(out[name].shape)
        drawn = base * np.exp(spread * noise) if base else spread * noise
        out[name] = jnp.asarray(drawn.astype(out[name].dtype))
    for name, factor in factors.items():
        out[name] = (out[name] * factor).astype(out[name].dtype)
    return out
```

```python
from contextlib import ExitStack

import concourse.bass as bass
from concourse import mybir

F32 = mybir.dt.float32
F16 = mybir.dt.float16
BF16 = mybir.dt.bfloat16
ALU = mybir.AluOpType
ACT = mybir.ActivationFunctionType
AX = mybir.AxisListType.X

P = 128
B, SEQ, D = 4, 256, 256
HEADS, DH = 16, 128
EXPERTS, TOP_K = 64, 8
KD = D // P
TILES = B * SEQ // P
UNITS = B * HEADS
ITER = 8
LAST = UNITS // ITER - 1
WCOLS = 3 * D + D
QW, KW, VW, OW = 0, D, 2 * D, 3 * D
STAGE = 8
EPS = 1e-5
NEG = -1.0e9

X_SCALE = 8.0
W_SCALE = 64.0
QKV_DOWN = 0.125
QKV_SCALE = X_SCALE * W_SCALE * QKV_DOWN
P_SCALE = 16384.0
Z_DOWN = 1.0 / 16384.0
A_SCALE = QKV_SCALE * W_SCALE
S_SCALE = float(DH) ** -0.5 / QKV_SCALE ** 2
MASK = NEG / S_SCALE


def is_int(v):
    return isinstance(v, int)


def positive(count):
    return not is_int(count) or count > 0


def in_register(eng, count):
    return count if is_int(count) else eng.to_reg(count)


def layer_kernel(nc, x, weights, router_w, router_b, expert_b, out):
    x_dram = x.rearrange("(t p) d -> p t d", p=P)
    out_dram = out.rearrange("(t p) d -> p t d", p=P)

    with ExitStack() as ctx:
        def sb(name, shape, dt):
            return ctx.enter_context(nc.sbuf_tensor(name, shape, dt))

        def pb(name, cols=512):
            return ctx.enter_context(nc.psum_tensor(name, [P, cols], F32))

        def sem(name):
            return ctx.enter_context(nc.semaphore(name))

        x_sb = sb("x_sb", [P, TILES, D], F32)
        w_raw = sb("w_raw", [P, STAGE, WCOLS], F32)
        w_hi = sb("w_hi", [P, HEADS, WCOLS], F16)
        w_lo = sb("w_lo", [P, HEADS, WCOLS], F16)
        xT_hi = sb("xT_hi", [P, KD, TILES * P], F16)
        xT_lo = sb("xT_lo", [P, KD, TILES * P], F16)
        xn = sb("xn", [P, 2, D], F32)
        qk_hi = sb("qk_hi", [P, 2, 2 * SEQ], F16)
        qk_lo = sb("qk_lo", [P, 2, 2 * SEQ], F16)
        v_hi = sb("v_hi", [P, 2, 2, 2, DH], F16)
        v_lo = sb("v_lo", [P, 2, 2, 2, DH], F16)
        probs = sb("probs", [P, 2, 3 * P], F32)
        pT_hi = sb("pT_hi", [P, 2, 3 * P], F16)
        pT_lo = sb("pT_lo", [P, 2, 3 * P], F16)
        z_hi = sb("z_hi", [P, 2, SEQ], F16)
        z_lo = sb("z_lo", [P, 2, SEQ], F16)
        row_max = sb("row_max", [P, 2, 2], F32)
        neg_max = sb("neg_max", [P, 2, 2], F32)
        row_sum = sb("row_sum", [P, 2, 2], F32)
        inv_sum = sb("inv_sum", [P, 2, 2], F32)
        attn = sb("attn", [P, TILES, D], F32)
        out_sb = sb("out_sb", [P, TILES, D], F32)
        ident = sb("ident", [P, P], F32)
        ident_b = sb("ident_b", [P, P], BF16)
        mask_b = sb("mask_b", [P, 2, P], BF16)
        minus_half = sb("minus_half", [P, 1], F32)
        rw_sb = sb("rw_sb", [P, KD, EXPERTS], F32)
        rb_sb = sb("rb_sb", [P, EXPERTS], F32)
        eb_sb = sb("eb_sb", [EXPERTS, D], F32)
        norm_of = {}
        for who in ["x"] + [f"{s}{lane}" for s in ("attn", "mid", "mix") for lane in (0, 1)]:
            norm_of[who] = (sb(f"bn6_{who}", [P, 6], F32), sb(f"mv_{who}", [P, 2], F32),
                            sb(f"var_{who}", [P, 1], F32), sb(f"rstd_{who}", [P, 1], F32))
        lanes = range(2)
        attn_n = [sb(f"attn_n{i}", [P, D], F32) for i in lanes]
        x_mid = [sb(f"x_mid{i}", [P, D], F32) for i in lanes]
        h_sb = [sb(f"h_sb{i}", [P, D], F32) for i in lanes]
        hT = [sb(f"hT{i}", [P, KD, P], F32) for i in lanes]
        logit = [sb(f"logit{i}", [P, EXPERTS], F32) for i in lanes]
        logit_nmax = [sb(f"logit_nmax{i}", [P, 1], F32) for i in lanes]
        expo = [sb(f"expo{i}", [P, EXPERTS], F32) for i in lanes]
        expo_sum = [sb(f"expo_sum{i}", [P, 1], F32) for i in lanes]
        expo_inv = [sb(f"expo_inv{i}", [P, 1], F32) for i in lanes]
        score = [sb(f"score{i}", [P, EXPERTS], F32) for i in lanes]
        top = [sb(f"top{i}", [P, TOP_K], F32) for i in lanes]
        struck = [sb(f"struck{i}", [P, EXPERTS], F32) for i in lanes]
        chosen = [sb(f"chosen{i}", [P, P], F32) for i in lanes]
        top_sum = [sb(f"top_sum{i}", [P, 1], F32) for i in lanes]
        chosenT = [sb(f"chosenT{i}", [P, P], F32) for i in lanes]
        y_sb = [sb(f"y_sb{i}", [P, D], F32) for i in lanes]
        y_n = [sb(f"y_n{i}", [P, D], F32) for i in lanes]

        qk_ps = pb("qk_ps")
        v_ps = pb("v_ps")
        s_ps = pb("s_ps")
        pT_ps = pb("pT_ps")
        z_ps = pb("z_ps")
        o_ps = pb("o_ps")
        aux_ps = [pb("aux_ps0"), pb("aux_ps1")]

        x_loaded = [sem(f"x_loaded{b}") for b in range(B)]
        w_loaded = [sem(f"w_loaded{h}") for h in range(HEADS)]
        small_loaded = sem("small_loaded")
        out_stored = sem("out_stored")
        consts_cleared = sem("consts_cleared")
        consts_ready = sem("consts_ready")
        attn_cleared = sem("attn_cleared")
        w_hi_by_pool = sem("w_hi_by_pool")
        probs_scaled = sem("probs_scaled")
        mid_ready = sem("mid_ready")
        y_normed = sem("y_normed")
        out_ready = sem("out_ready")
        w_hi_by_act = sem("w_hi_by_act")
        x_hi_done = sem("x_hi_done")
        qk_hi_done = sem("qk_hi_done")
        v_hi_done = sem("v_hi_done")
        probs_exped = sem("probs_exped")
        pT_hi_done = sem("pT_hi_done")
        z_hi_done = sem("z_hi_done")
        hT_ready = sem("hT_ready")
        expo_ready = sem("expo_ready")
        chosenT_ready = sem("chosenT_ready")
        w_split = sem("w_split")
        x_normed = sem("x_normed")
        x_split = sem("x_split")
        qk_split = sem("qk_split")
        v_split = sem("v_split")
        max_found = sem("max_found")
        neg_max_ready = sem("neg_max_ready")
        sums_inverted = sem("sums_inverted")
        pT_split = sem("pT_split")
        z_split = sem("z_split")
        attn_added = sem("attn_added")
        attn_normed = sem("attn_normed")
        h_ready = sem("h_ready")
        logit_biased = sem("logit_biased")
        logit_max_found = sem("logit_max_found")
        expo_inverted = sem("expo_inverted")
        score_ready = sem("score_ready")
        top_found = sem("top_found")
        top_struck = sem("top_struck")
        chosen_ready = sem("chosen_ready")
        top_summed = sem("top_summed")
        y_ready = sem("y_ready")
        stats_of = {s: sem(f"stats_{s}") for s in ("x", "attn", "mid", "mix")}
        moments_of = {s: sem(f"moments_{s}") for s in ("x", "attn", "mid", "mix")}
        var_of = {s: sem(f"var_{s}_ready") for s in ("x", "attn", "mid", "mix")}
        rstd_of = {s: sem(f"rstd_{s}_ready") for s in ("x", "attn", "mid", "mix")}
        x_turned = sem("x_turned")
        qk_projected = sem("qk_projected")
        v_projected = sem("v_projected")
        scores_ready = sem("scores_ready")
        probs_turned = sem("probs_turned")
        z_summed = sem("z_summed")
        o_summed = sem("o_summed")
        h_turned = sem("h_turned")
        logits_ready = sem("logits_ready")
        chosen_turned = sem("chosen_turned")
        mix_ready = sem("mix_ready")

        block = ctx.enter_context(nc.Block())

        def all_units(eng, unit):
            for U in (-2, -1):
                unit(U // ITER, U % ITER)
            for t in (0, 1):
                for k in range(ITER):
                    unit(t, k)
            with eng.Fori(2, LAST) as t:
                for k in range(ITER):
                    unit(t, k)
            for k in range(ITER):
                unit(LAST, k)
            unit(LAST + 1, 0)

        def exists(t, k, ahead):
            return not is_int(t) or 0 <= ITER * t + k + ahead < UNITS

        def number(t, k, ahead=0):
            return t * ITER + (k + ahead)

        def pair_number(t, k):
            return t * (ITER // 2) + k // 2

        X_TILE_AT = {2 * (i - 1): i for i in range(2, TILES)}

        def moments(dve, who, lane, src, count):
            bn6, mv, _, _ = norm_of[who if who == "x" else f"{who}{lane}"]
            nc.vector.bn_stats(bn6[:, :], src).then_inc(stats_of[who], 1)
            n = in_register(dve, count)
            dve.wait_ge(x_loaded[0], 16)
            dve.wait_ge(stats_of[who], n)
            nc.vector.bn_aggr(mv[:, :], bn6[:, :]).then_inc(moments_of[who], 1)

        def inverse_deviation(pool, who, lane, eps, scale, count):
            _, mv, var, rstd = norm_of[who if who == "x" else f"{who}{lane}"]
            n = in_register(pool, count)
            pool.wait_ge(consts_ready, 2)
            pool.wait_ge(moments_of[who], n)
            nc.gpsimd.tensor_scalar(var[:, :], mv[:, 1:2], eps, scale, ALU.add, ALU.mult).then_inc(var_of[who], 1)
            pool.wait_ge(var_of[who], count)
            nc.gpsimd.tensor_tensor(rstd[:, :], var[:, :], minus_half[:, :], ALU.pow).then_inc(rstd_of[who], 1)

        def normalised(dve, who, lane, dst, src, count, done):
            _, mv, _, rstd = norm_of[who if who == "x" else f"{who}{lane}"]
            dve.wait_ge(rstd_of[who], count)
            nc.vector.tensor_scalar(dst, src, mv[:, 0:1], rstd[:, 0:1], ALU.subtract, ALU.mult).then_inc(done, 1)

        @block.sync
        def _(sp):
            sp.dma_start(x_sb[:, 0:2, :], x_dram[:, 0:2, :]).then_inc(x_loaded[0], 16)
            for h in range(HEADS):
                if h >= STAGE:
                    sp.wait_ge(w_split, h - STAGE + 1)
                sp.dma_start(w_raw[:, h % STAGE, :], weights[h]).then_inc(w_loaded[h], 16)
                if 1 <= h < B:
                    sp.dma_start(x_sb[:, 2 * h:2 * h + 2, :], x_dram[:, 2 * h:2 * h + 2, :]).then_inc(x_loaded[h], 16)
                if h == B:
                    sp.dma_start(rw_sb[:, :, :], router_w).then_inc(small_loaded, 16)
                    sp.dma_start(rb_sb[:, :], router_b).then_inc(small_loaded, 16)
                    sp.dma_start(eb_sb[:, :], expert_b).then_inc(small_loaded, 16)
            with sp.Fori(0, TILES) as e:
                sp.wait_ge(out_ready, e + 1)
                sp.dma_start(out_dram[:, bass.ds(e, 1), :], out_sb[:, bass.ds(e, 1), :]).then_inc(out_stored, 16)
            sp.wait_ge(out_stored, 16 * TILES)

        @block.gpsimd
        def _(pool):
            nc.gpsimd.memset(ident[:, :], 0.0).then_inc(consts_cleared, 1)
            nc.gpsimd.memset(minus_half[:, :], -0.5).then_inc(consts_ready, 1)
            pool.wait_ge(consts_cleared, 1)
            nc.gpsimd.affine_select(out=ident[:, :], in_=ident[:, :], compare_op=ALU.not_equal, fill=1.0, base=0,
                                    pattern=[[-1, P]], channel_multiplier=1).then_inc(consts_ready, 1)
            pool.wait_ge(consts_ready, 1)

            def token_rstd(i):
                inverse_deviation(pool, "x", 0, EPS, X_SCALE ** -2, i + 1)

            token_rstd(0)
            token_rstd(1)
            nc.gpsimd.memset(ident_b[:, :], 0.0).then_inc(consts_cleared, 1)
            nc.gpsimd.memset(mask_b[:, :, :], 0.0).then_inc(consts_cleared, 1)
            pool.wait_ge(consts_cleared, 3)
            nc.gpsimd.affine_select(out=ident_b[:, :], in_=ident_b[:, :], compare_op=ALU.not_equal, fill=1.0, base=0,
                                    pattern=[[-1, P]], channel_multiplier=1).then_inc(consts_ready, 1)
            nc.gpsimd.affine_select(out=mask_b[:, :, :], in_=mask_b[:, :, :], compare_op=ALU.is_ge, fill=MASK, base=0,
                                    pattern=[[0, 2], [-1, P]], channel_multiplier=1).then_inc(consts_ready, 1)
            nc.gpsimd.memset(attn[:, :, :], 0.0).then_inc(attn_cleared, 1)
            for lane in lanes:
                nc.gpsimd.memset(chosen[lane][:, :], 0.0).then_inc(attn_cleared, 1)

            def finish(lane, e, step):
                if step == 0:
                    inverse_deviation(pool, "attn", lane, EPS * A_SCALE ** 2, 1.0, e + 1)
                if step == 1:
                    pool.wait_ge(attn_normed, e + 1)
                    nc.gpsimd.tensor_tensor(x_mid[lane][:, :], attn_n[lane][:, :], x_sb[:, e, :],
                                            ALU.add).then_inc(mid_ready, 1)
                if step == 2:
                    inverse_deviation(pool, "mid", lane, EPS, 1.0, e + 1)
                if step == 3:
                    inverse_deviation(pool, "mix", lane, EPS, 1.0, e + 1)
                if step == 4:
                    _, mv, _, rstd = norm_of[f"mix{lane}"]
                    n = in_register(pool, e + 1)
                    pool.wait_ge(consts_ready, 2)
                    pool.wait_ge(rstd_of["mix"], n)
                    nc.gpsimd.tensor_scalar(y_n[lane][:, :], y_sb[lane][:, :], mv[:, 0:1], rstd[:, 0:1],
                                            ALU.subtract, ALU.mult).then_inc(y_normed, 1)
                    pool.wait_ge(y_normed, e + 1)
                    nc.gpsimd.tensor_tensor(out_sb[:, e, :], y_n[lane][:, :], x_mid[lane][:, :],
                                            ALU.add).then_inc(out_ready, 1)

            def unit(t, k):
                U = number(t, k)
                if exists(t, k, 1):
                    n = in_register(pool, U + 2)
                    pool.wait_ge(consts_ready, 2)
                    pool.wait_ge(sums_inverted, n)
                    s = (k + 1) % 2
                    nc.gpsimd.tensor_scalar(probs[:, s, 0:P], probs[:, s, 0:P], inv_sum[:, s, 0:1], P_SCALE,
                                            ALU.mult, ALU.mult)
                    nc.gpsimd.tensor_scalar(probs[:, s, P:3 * P], probs[:, s, P:3 * P], inv_sum[:, s, 1:2], P_SCALE,
                                            ALU.mult, ALU.mult).then_inc(probs_scaled, 1)
                if is_int(t) and 4 <= U + 4 < HEADS:
                    h = U + 4
                    pool.wait_ge(w_loaded[h], 16)
                    nc.gpsimd.tensor_scalar(w_hi[:, h, :], w_raw[:, h % STAGE, :], W_SCALE, 1.0,
                                            ALU.mult, ALU.mult).then_inc(w_hi_by_pool, 1)
                if is_int(t) and U in X_TILE_AT:
                    token_rstd(X_TILE_AT[U])
                if not is_int(t) or 2 <= t <= LAST:
                    for at, step in ((2, 0), (2, 1), (3, 2), (7, 3), (7, 4)):
                        if k == at:
                            finish(0, t - 2, step)

            all_units(pool, unit)
            for step in range(5):
                for lane in lanes:
                    finish(lane, TILES - 2 + lane, step)

        @block.scalar
        def _(act):
            def weights_high(h):
                act.wait_ge(w_loaded[h], 16)
                nc.scalar.activation(w_hi[:, h, :], w_raw[:, h, :], ACT.Copy, scale=W_SCALE).then_inc(w_hi_by_act, 1)

            def tokens_high(i):
                act.wait_ge(x_turned, i + 1)
                nc.scalar.activation(xT_hi[:, :, i * P:(i + 1) * P],
                                     aux_ps[i % 2][:, 0:D].rearrange("p (c n) -> p c n", c=KD),
                                     ACT.Copy).then_inc(x_hi_done, 1)

            def finish(lane, e, step):
                if step == 0:
                    act.wait_ge(h_turned, e + 1)
                    nc.scalar.activation(hT[lane][:, :, :], aux_ps[lane][:, 0:D].rearrange("p (c n) -> p c n", c=KD),
                                         ACT.Copy).then_inc(hT_ready, 1)
                if step == 1:
                    act.wait_ge(logit_max_found, e + 1)
                    nc.scalar.activation(expo[lane][:, :], logit[lane][:, :], ACT.Exp, bias=logit_nmax[lane][:, :],
                                         accum_out=expo_sum[lane][:, :]).then_inc(expo_ready, 1)
                if step == 2:
                    act.wait_ge(chosen_turned, e + 1)
                    nc.scalar.activation(chosenT[lane][:, :], aux_ps[lane][:, 320:320 + P],
                                         ACT.Copy).then_inc(chosenT_ready, 1)

            def unit(t, k):
                U = number(t, k)
                if exists(t, k, -1):
                    act.wait_ge(z_summed, U)
                    nc.scalar.activation(z_hi[:, (k + 1) % 2, :], z_ps[:, 0:SEQ], ACT.Copy,
                                         scale=Z_DOWN).then_inc(z_hi_done, 1)
                if exists(t, k, 0):
                    act.wait_ge(probs_turned, U + 1)
                    nc.scalar.activation(pT_hi[:, k % 2, :], pT_ps[:, 0:3 * P], ACT.Copy).then_inc(pT_hi_done, 1)
                if exists(t, k, 1):
                    act.wait_ge(neg_max_ready, U + 2)
                    s = (k + 1) % 2
                    nc.scalar.activation(probs[:, s, 0:P], s_ps[:, 0:P], ACT.Exp, bias=neg_max[:, s, 0:1],
                                         scale=S_SCALE, accum_out=row_sum[:, s, 0:1])
                    nc.scalar.activation(probs[:, s, P:3 * P], s_ps[:, P:3 * P], ACT.Exp, bias=neg_max[:, s, 1:2],
                                         scale=S_SCALE, accum_out=row_sum[:, s, 1:2]).then_inc(probs_exped, 1)
                if is_int(t) and U - 2 in X_TILE_AT:
                    tokens_high(X_TILE_AT[U - 2])
                if exists(t, k, 2):
                    act.wait_ge(qk_projected, U + 3)
                    nc.scalar.activation(qk_hi[:, k % 2, :], qk_ps[:, :], ACT.Copy,
                                         scale=QKV_DOWN).then_inc(qk_hi_done, 1)
                if k % 2 and exists(t, k, 1):
                    act.wait_ge(v_projected, pair_number(t, k) + 2)
                    nc.scalar.activation(v_hi[:, (k // 2 + 1) % 2, :, :, :],
                                         v_ps[:, :].rearrange("p (m h n) -> p m h n", m=2, h=2), ACT.Copy,
                                         scale=QKV_DOWN).then_inc(v_hi_done, 1)
                if is_int(t) and U < 0:
                    weights_high(U + 4)
                if not is_int(t) or 2 <= t <= LAST:
                    for at, step in ((4, 0), (5, 1), (7, 2)):
                        if k == at:
                            finish(0, t - 2, step)

            weights_high(0)
            weights_high(1)
            tokens_high(0)
            tokens_high(1)
            all_units(act, unit)
            for step in range(3):
                for lane in lanes:
                    finish(lane, TILES - 2 + lane, step)

        @block.vector
        def _(dve):
            def weights_low(h, high_done, count):
                dve.wait_ge(high_done, count)
                nc.vector.scalar_tensor_tensor(out=w_lo[:, h, :], in0=w_raw[:, h % STAGE, :], scalar=W_SCALE,
                                               in1=w_hi[:, h, :], op0=ALU.mult, op1=ALU.subtract).then_inc(w_split, 1)

            def token_moments(i):
                dve.wait_ge(x_loaded[i // 2], 16)
                moments(dve, "x", 0, x_sb[:, i, :], i + 1)

            def token_normalise(i):
                normalised(dve, "x", 0, xn[:, i % 2, :], x_sb[:, i, :], i + 1, x_normed)

            def tokens_low(i):
                dve.wait_ge(x_hi_done, i + 1)
                nc.vector.scalar_tensor_tensor(out=xT_lo[:, :, i * P:(i + 1) * P],
                                               in0=aux_ps[i % 2][:, 0:D].rearrange("p (c n) -> p c n", c=KD),
                                               scalar=1.0, in1=xT_hi[:, :, i * P:(i + 1) * P],
                                               op0=ALU.mult, op1=ALU.subtract).then_inc(x_split, 1)

            def add_attention(t):
                dve.wait_ge(o_summed, t)
                first = (t - 1) // 2 * 2
                tiles = attn[:, bass.ds(first, 2), :]
                nc.vector.tensor_tensor(tiles, o_ps[:, :].rearrange("p (a d) -> p a d", a=2), tiles,
                                        ALU.add).then_inc(attn_added, 1)

            def finish(lane, e, step):
                if step == 0:
                    moments(dve, "attn", lane, attn[:, e, :], e + 1)
                if step == 1:
                    normalised(dve, "attn", lane, attn_n[lane][:, :], attn[:, e, :], e + 1, attn_normed)
                if step == 2:
                    dve.wait_ge(mid_ready, e + 1)
                    moments(dve, "mid", lane, x_mid[lane][:, :], e + 1)
                if step == 3:
                    normalised(dve, "mid", lane, h_sb[lane][:, :], x_mid[lane][:, :], e + 1, h_ready)
                if step == 4:
                    dve.wait_ge(small_loaded, 16 * 3)
                    dve.wait_ge(logits_ready, e + 1)
                    nc.vector.tensor_tensor(logit[lane][:, :], aux_ps[lane][:, D:D + EXPERTS], rb_sb[:, :],
                                            ALU.add).then_inc(logit_biased, 1)
                    dve.wait_ge(logit_biased, e + 1)
                    nc.vector.tensor_reduce(logit_nmax[lane][:, :], logit[lane][:, :], AX, ALU.max,
                                            negate=True).then_inc(logit_max_found, 1)
                if step == 5:
                    dve.wait_ge(expo_ready, e + 1)
                    nc.vector.reciprocal(expo_inv[lane][:, :], expo_sum[lane][:, :]).then_inc(expo_inverted, 1)
                    dve.wait_ge(expo_inverted, e + 1)
                    nc.vector.tensor_scalar(score[lane][:, :], expo[lane][:, :], expo_inv[lane][:, 0:1], None,
                                            ALU.mult).then_inc(score_ready, 1)
                    n = in_register(dve, e + 1)
                    dve.wait_ge(x_loaded[0], 16)
                    dve.wait_ge(score_ready, n)
                    nc.vector.max(top[lane][:, :], score[lane][:, :]).then_inc(top_found, 1)
                    n = in_register(dve, e + 1)
                    dve.wait_ge(x_loaded[0], 16)
                    dve.wait_ge(top_found, n)
                    nc.vector.match_replace(struck[lane][:, :], top[lane][:, :], score[lane][:, :],
                                            -1.0).then_inc(top_struck, 1)
                    nc.vector.reduce_sum(top_sum[lane][:, :], top[lane][:, :], AX).then_inc(top_summed, 1)
                    dve.wait_ge(top_struck, e + 1)
                    nc.vector.scalar_tensor_tensor(out=chosen[lane][:, 0:EXPERTS], in0=struck[lane][:, :], scalar=0.0,
                                                   in1=score[lane][:, :], op0=ALU.is_lt,
                                                   op1=ALU.mult).then_inc(chosen_ready, 1)
                if step == 6:
                    dve.wait_ge(mix_ready, e + 1)
                    dve.wait_ge(top_summed, e + 1)
                    nc.vector.scalar_tensor_tensor(out=y_sb[lane][:, :], in0=h_sb[lane][:, :],
                                                   scalar=top_sum[lane][:, 0:1], in1=aux_ps[lane][:, 0:D],
                                                   op0=ALU.mult, op1=ALU.add).then_inc(y_ready, 1)
                    dve.wait_ge(y_ready, e + 1)
                    moments(dve, "mix", lane, y_sb[lane][:, :], e + 1)

            def unit(t, k):
                U = number(t, k)
                in_finish = not is_int(t) or 2 <= t <= LAST
                if exists(t, k, -1):
                    dve.wait_ge(z_hi_done, U)
                    nc.vector.scalar_tensor_tensor(out=z_lo[:, (k + 1) % 2, :], in0=z_ps[:, 0:SEQ], scalar=Z_DOWN,
                                                   in1=z_hi[:, (k + 1) % 2, :], op0=ALU.mult,
                                                   op1=ALU.subtract).then_inc(z_split, 1)
                if exists(t, k, 1):
                    s = (k + 1) % 2
                    dve.wait_ge(scores_ready, U + 2)
                    nc.vector.tensor_reduce(row_max[:, s, 0:1], s_ps[:, 0:P], AX, ALU.max)
                    nc.vector.tensor_reduce(row_max[:, s, 1:2], s_ps[:, P:3 * P], AX, ALU.max).then_inc(max_found, 1)
                    dve.wait_ge(max_found, U + 2)
                    nc.vector.tensor_scalar(neg_max[:, s, :], row_max[:, s, :], -S_SCALE, None,
                                            ALU.mult).then_inc(neg_max_ready, 1)
                if is_int(t):
                    if U - 2 in X_TILE_AT:
                        tokens_low(X_TILE_AT[U - 2])
                    if U - 1 in X_TILE_AT:
                        token_normalise(X_TILE_AT[U - 1])
                if in_finish:
                    for at, step in ((3, 2), (4, 3)):
                        if k == at:
                            finish(0, t - 2, step)
                if exists(t, k, 0):
                    dve.wait_ge(pT_hi_done, U + 1)
                    nc.vector.scalar_tensor_tensor(out=pT_lo[:, k % 2, :], in0=pT_ps[:, 0:3 * P], scalar=1.0,
                                                   in1=pT_hi[:, k % 2, :], op0=ALU.mult,
                                                   op1=ALU.subtract).then_inc(pT_split, 1)
                if exists(t, k, 1):
                    dve.wait_ge(probs_exped, U + 2)
                    nc.vector.reciprocal(inv_sum[:, s, :], row_sum[:, s, :]).then_inc(sums_inverted, 1)
                if exists(t, k, 2):
                    dve.wait_ge(qk_hi_done, U + 3)
                    nc.vector.scalar_tensor_tensor(out=qk_lo[:, k % 2, :], in0=qk_ps[:, :], scalar=QKV_DOWN,
                                                   in1=qk_hi[:, k % 2, :], op0=ALU.mult,
                                                   op1=ALU.subtract).then_inc(qk_split, 1)
                if k % 2 and exists(t, k, 1):
                    dve.wait_ge(v_hi_done, pair_number(t, k) + 2)
                    s = (k // 2 + 1) % 2
                    nc.vector.scalar_tensor_tensor(out=v_lo[:, s, :, :, :].rearrange("p m h n -> p (m h n)"),
                                                   in0=v_ps[:, :], scalar=QKV_DOWN,
                                                   in1=v_hi[:, s, :, :, :].rearrange("p m h n -> p (m h n)"),
                                                   op0=ALU.mult, op1=ALU.subtract).then_inc(v_split, 1)
                if is_int(t) and U < 0:
                    weights_low(U + 4, w_hi_by_act, U + 5)
                if is_int(t) and 4 <= U + 4 < HEADS:
                    weights_low(U + 4, w_hi_by_pool, U + 1)
                if is_int(t) and U in X_TILE_AT:
                    token_moments(X_TILE_AT[U])
                if k == 0 and not (is_int(t) and t < 1):
                    if is_int(t) and t == 1:
                        dve.wait_ge(attn_cleared, 3)
                    add_attention(t)
                if in_finish:
                    for at, step in ((2, 0), (2, 1), (5, 4), (6, 5), (7, 6)):
                        if k == at:
                            if step == 0:
                                dve.wait_ge(attn_added, t)
                            finish(0, t - 2, step)

            for i in (0, 1):
                token_moments(i)
                token_normalise(i)
            weights_low(0, w_hi_by_act, 1)
            weights_low(1, w_hi_by_act, 2)
            tokens_low(0)
            tokens_low(1)
            all_units(dve, unit)
            dve.wait_ge(attn_added, LAST + 1)
            for step in range(7):
                for lane in lanes:
                    finish(lane, TILES - 2 + lane, step)

        @block.tensor
        def _(pe):
            SPLIT = ((0, 0), (0, 1), (1, 0))
            w = (w_hi, w_lo)
            xT = (xT_hi, xT_lo)
            qk = (qk_hi, qk_lo)
            v = (v_hi, v_lo)
            pT = (pT_hi, pT_lo)
            z = (z_hi, z_lo)

            def place(t, k, ahead, half, batch, next_half, next_batch):
                if is_int(t):
                    return (ITER * t + k + ahead) % HEADS, (ITER * t + k + ahead) // HEADS
                if k + ahead < 0:
                    return next_half * ITER + (k + ahead + ITER), None
                if k + ahead < ITER:
                    return half * ITER + (k + ahead), batch
                return next_half * ITER + (k + ahead - ITER), next_batch

            def tokens_turn(i):
                pe.wait_ge(x_normed, i + 1)
                for c in range(KD):
                    last = nc.tensor.transpose(aux_ps[i % 2][:, c * P:(c + 1) * P], xn[:, i % 2, c * P:(c + 1) * P],
                                               ident[:, :])
                last.then_inc(x_turned, 1)

            def finish(lane, e, step):
                if step == 0:
                    pe.wait_ge(h_ready, e + 1)
                    for c in range(KD):
                        last = nc.tensor.transpose(aux_ps[lane][:, c * P:(c + 1) * P],
                                                   h_sb[lane][:, c * P:(c + 1) * P], ident[:, :])
                    last.then_inc(h_turned, 1)
                if step == 1:
                    pe.wait_ge(hT_ready, e + 1)
                    for c in range(KD):
                        last = nc.tensor.matmul(aux_ps[lane][:, D:D + EXPERTS], hT[lane][:, c, :], rw_sb[:, c, :],
                                                start=(c == 0), stop=(c == KD - 1))
                    last.then_inc(logits_ready, 1)
                if step == 2:
                    pe.wait_ge(chosen_ready, e + 1)
                    nc.tensor.transpose(aux_ps[lane][:, 320:320 + P], chosen[lane][:, :],
                                        ident[:, :]).then_inc(chosen_turned, 1)
                if step == 3:
                    pe.wait_ge(chosenT_ready, e + 1)
                    nc.tensor.matmul(aux_ps[lane][:, 0:D], chosenT[lane][0:EXPERTS, :], eb_sb[:, :],
                                     start=True, stop=True).then_inc(mix_ready, 1)

            def unit(t, k):
                U = number(t, k)
                if is_int(t):
                    half = batch = next_half = next_batch = None
                else:
                    half, batch, next_half, next_batch = regs
                where = (half, batch, next_half, next_batch)

                if exists(t, k, 1):
                    pe.wait_ge(qk_split, U + 2)
                    if positive(U + 1):
                        pe.wait_ge(probs_exped, U + 1)
                    s = (k + 1) % 2
                    diagonals = s_ps[:, :].rearrange("p (a b) -> p a b", b=2 * P)[:, :, 0:P]
                    nc.tensor.matmul(diagonals, ident_b[:, :], mask_b[:, :, :], start=True, stop=False,
                                     skip_group_check=True)
                    for i, j in SPLIT:
                        nc.tensor.matmul(s_ps[:, 0:P], qk[i][:, s, 0:P], qk[j][:, s, SEQ:SEQ + P],
                                         start=False, stop=(i == 1), skip_group_check=True)
                    for i, j in SPLIT:
                        last = nc.tensor.matmul(s_ps[:, P:3 * P], qk[i][:, s, P:2 * P], qk[j][:, s, SEQ:2 * SEQ],
                                                start=False, stop=(i == 1), skip_group_check=True)
                    last.then_inc(scores_ready, 1)
                if exists(t, k, 0):
                    pe.wait_ge(probs_scaled, U + 1)
                    if positive(U):
                        pe.wait_ge(pT_split, U)
                    for n in range(3):
                        last = nc.tensor.transpose(pT_ps[:, n * P:(n + 1) * P], probs[:, k % 2, n * P:(n + 1) * P],
                                                   ident[:, :])
                    last.then_inc(probs_turned, 1)
                if not is_int(t) or 2 <= t <= LAST:
                    for at, step in ((5, 1), (7, 2)):
                        if k == at:
                            finish(0, t - 2, step)
                if exists(t, k, 2):
                    h, b = place(t, k, 2, *where)
                    if is_int(t):
                        pe.wait_ge(w_split, min(h + 1, HEADS) if U + 2 < HEADS else HEADS)
                        pe.wait_ge(x_split, 2 * (b + 1))
                    cols = bass.ds(b * SEQ, SEQ)
                    for part, base in ((0, QW), (1, KW)):
                        n = 0
                        for i, j in SPLIT:
                            for c in range(KD):
                                last = nc.tensor.matmul(qk_ps[:, part * SEQ:(part + 1) * SEQ],
                                                        w[i][:, h, base + c * P:base + (c + 1) * P],
                                                        xT[j][:, c, cols], start=(n == 0), stop=(n == 5))
                                n += 1
                    last.then_inc(qk_projected, 1)
                if exists(t, k, -1):
                    pe.wait_ge(z_split, U)
                    if k == 1 and positive(t):
                        pe.wait_ge(attn_added, t)
                    h, _ = place(t, k, -1, *where)
                    s = (k + 1) % 2
                    for a in range(2):
                        for n, (i, j) in enumerate(SPLIT):
                            last = nc.tensor.matmul(o_ps[:, a * D:(a + 1) * D], z[i][:, s, a * P:(a + 1) * P],
                                                    w[j][:, h, OW:OW + D], start=(k == 1 and a == 0 and n == 0),
                                                    stop=(k == 0), skip_group_check=True)
                    if k == 0:
                        last.then_inc(o_summed, 1)
                if exists(t, k, 2 - k % 2):
                    h, b = place(t, k, 2 - k % 2, *where)
                    a = k % 2
                    if a == 0 and positive(pair_number(t, k) + 1):
                        pe.wait_ge(v_split, pair_number(t, k) + 1)
                    if is_int(t) and U + 2 < HEADS:
                        pe.wait_ge(w_split, h + 2)
                    n = 0
                    for i, j in SPLIT:
                        for c in range(KD):
                            last = nc.tensor.matmul(v_ps[:, a * 2 * DH:(a + 1) * 2 * DH],
                                                    xT[i][:, c, bass.ds(b * SEQ + a * P, P)],
                                                    w[j][:, bass.ds(h, 2), VW + c * P:VW + (c + 1) * P],
                                                    start=(n == 0), stop=(n == 5))
                            n += 1
                    if a == 1:
                        last.then_inc(v_projected, 1)
                if is_int(t) and U - 1 in X_TILE_AT:
                    tokens_turn(X_TILE_AT[U - 1])
                if not is_int(t) or 2 <= t <= LAST:
                    for at, step in ((4, 0), (7, 3)):
                        if k == at:
                            finish(0, t - 2, step)
                if exists(t, k, 0):
                    pe.wait_ge(pT_split, U + 1)
                    pe.wait_ge(v_split, pair_number(t, k) + 1)
                    g, hh, s = k // 2 % 2, k % 2, k % 2
                    for n, (i, j) in enumerate(SPLIT):
                        nc.tensor.matmul(z_ps[:, 0:SEQ], v[i][:, g, 0, hh, :], pT[j][:, s, 0:SEQ],
                                         start=(n == 0), stop=False, skip_group_check=True)
                    for n, (i, j) in enumerate(SPLIT):
                        last = nc.tensor.matmul(z_ps[:, P:SEQ], v[i][:, g, 1, hh, :], pT[j][:, s, SEQ:3 * P],
                                                start=False, stop=(n == 2), skip_group_check=True)
                    last.then_inc(z_summed, 1)

            pe.wait_ge(consts_ready, 2)
            tokens_turn(0)
            tokens_turn(1)
            pe.wait_ge(consts_ready, 4)
            regs = None
            for U in (-2, -1):
                unit(-1, U % ITER)
            for t in (0, 1):
                for k in range(ITER):
                    unit(t, k)
            with pe.Fori(2, LAST) as t:
                regs = (pe.snap(t % 2), pe.snap(t // 2), pe.snap((t + 1) % 2), pe.snap((t + 1) // 2))
                for k in range(ITER):
                    unit(t, k)
            for k in range(ITER):
                unit(LAST, k)
            unit(LAST + 1, 0)
            for step in range(4):
                for lane in lanes:
                    finish(lane, TILES - 2 + lane, step)


def kernel(**inputs):
    import numpy as _np
    import concourse.bacc as _bacc
    from concourse.bass_utils import run_bass_kernel_spmd as _run

    x = _np.ascontiguousarray(inputs["L0_attn_x"]).reshape(B * SEQ, D)

    def head_rows(w):
        w = _np.asarray(w).transpose(0, 2, 1).reshape(HEADS, KD, P, DH)
        return w.transpose(0, 2, 1, 3).reshape(HEADS, P, KD * DH)

    w_o = _np.asarray(inputs["L0_attn_W_O"]).transpose(0, 2, 1)
    weights = _np.ascontiguousarray(_np.concatenate(
        [head_rows(inputs["L0_attn_W_Q"]), head_rows(inputs["L0_attn_W_K"]), head_rows(inputs["L0_attn_W_V"]), w_o],
        axis=2))
    router_w = _np.ascontiguousarray(
        _np.asarray(inputs["L0_ffn_router_weight"]).T.reshape(KD, P, EXPERTS).transpose(1, 0, 2))
    router_b = _np.ascontiguousarray(_np.broadcast_to(_np.asarray(inputs["L0_ffn_router_bias"]), (P, EXPERTS)))
    expert_b = _np.ascontiguousarray(inputs["L0_ffn_expert_bias"])

    nc = _bacc.Bacc("TRN2", target_bir_lowering=False, num_devices=1)
    arrays, args = {}, []
    for name, a in (("x", x), ("weights", weights), ("router_w", router_w), ("router_b", router_b),
                    ("expert_b", expert_b)):
        arrays[f"in_{name}_dram"] = a
        args.append(nc.dram_tensor(f"in_{name}_dram", a.shape, F32, kind="ExternalInput").ap())
    args.append(nc.dram_tensor("out_0_dram", (B * SEQ, D), F32, kind="ExternalOutput").ap())
    layer_kernel(nc, *args)
    r = _run(nc, [arrays], core_ids=[0])
    return r.results[0]["out_0_dram"].reshape(B, SEQ, D)
```

```python
from contextlib import ExitStack

import concourse.bass as bass
from concourse import mybir

F32 = mybir.dt.float32
F16 = mybir.dt.float16
BF16 = mybir.dt.bfloat16
ALU = mybir.AluOpType
ACT = mybir.ActivationFunctionType
AX = mybir.AxisListType.X

P = 128
B, SEQ, D = 4, 256, 256
HEADS, DH = 16, 128
EXPERTS, TOP_K = 64, 8
KD = D // P
TILES = B * SEQ // P
UNITS = B * HEADS
ITER = 8
LAST = UNITS // ITER - 1
WCOLS = 3 * D + D
QW, KW, VW, OW = 0, D, 2 * D, 3 * D
STAGE = 8
EARLY = 4
EPS = 1e-5
NEG = -1.0e9

X_SCALE = 8.0
W_SCALE = 64.0
QKV_DOWN = 0.125
QKV_SCALE = X_SCALE * W_SCALE * QKV_DOWN
P_SCALE = 16384.0
Z_DOWN = 1.0 / 16384.0
A_SCALE = QKV_SCALE * W_SCALE
S_SCALE = float(DH) ** -0.5 / QKV_SCALE ** 2
MASK = NEG / S_SCALE


def is_int(v):
    return isinstance(v, int)


def positive(count):
    return not is_int(count) or count > 0


def in_register(eng, count):
    return count if is_int(count) else eng.to_reg(count)


def layer_kernel(nc, x, weights, router_w, router_b, expert_b, out):
    x_dram = x.rearrange("(t p) d -> p t d", p=P)
    out_dram = out.rearrange("(t p) d -> p t d", p=P)

    with ExitStack() as ctx:
        def sb(name, shape, dt):
            return ctx.enter_context(nc.sbuf_tensor(name, shape, dt))

        def pb(name, cols=512):
            return ctx.enter_context(nc.psum_tensor(name, [P, cols], F32))

        def sem(name):
            return ctx.enter_context(nc.semaphore(name))

        x_sb = sb("x_sb", [P, TILES, D], F32)
        w_raw = sb("w_raw", [P, STAGE, WCOLS], F32)
        w_hi = sb("w_hi", [P, HEADS, WCOLS], F16)
        w_lo = sb("w_lo", [P, HEADS, WCOLS], F16)
        xT_hi = sb("xT_hi", [P, KD, TILES * P], F16)
        xT_lo = sb("xT_lo", [P, KD, TILES * P], F16)
        xn = sb("xn", [P, 2, D], F32)
        qk_hi = sb("qk_hi", [P, 2, 2 * SEQ], F16)
        qk_lo = sb("qk_lo", [P, 2, 2 * SEQ], F16)
        v_hi = sb("v_hi", [P, 2, 2, 2, DH], F16)
        v_lo = sb("v_lo", [P, 2, 2, 2, DH], F16)
        probs = sb("probs", [P, 2, 3 * P], F32)
        pT_hi = sb("pT_hi", [P, 2, 3 * P], F16)
        pT_lo = sb("pT_lo", [P, 2, 3 * P], F16)
        z_hi = sb("z_hi", [P, 2, SEQ], F16)
        z_lo = sb("z_lo", [P, 2, SEQ], F16)
        row_max = sb("row_max", [P, 2, 2], F32)
        neg_max = sb("neg_max", [P, 2, 2], F32)
        row_sum = sb("row_sum", [P, 2, 2], F32)
        inv_sum = sb("inv_sum", [P, 2, 2], F32)
        attn = sb("attn", [P, TILES, D], F32)
        out_sb = sb("out_sb", [P, TILES, D], F32)
        ident = sb("ident", [P, P], F32)
        ident_b = sb("ident_b", [P, P], BF16)
        mask_b = sb("mask_b", [P, 2, P], BF16)
        minus_half = sb("minus_half", [P, 1], F32)
        rw_sb = sb("rw_sb", [P, KD, EXPERTS], F32)
        rb_sb = sb("rb_sb", [P, EXPERTS], F32)
        eb_sb = sb("eb_sb", [EXPERTS, D], F32)
        norm_of = {}
        for who in ["x0", "x1"] + [f"{s}{lane}" for s in ("attn", "mid", "mix") for lane in (0, 1)]:
            norm_of[who] = (sb(f"bn6_{who}", [P, 6], F32), sb(f"mv_{who}", [P, 2], F32),
                            sb(f"var_{who}", [P, 1], F32), sb(f"rstd_{who}", [P, 1], F32))
        mix_shift = sb("mix_shift", [P, 1], F32)
        lanes = range(2)
        attn_n = [sb(f"attn_n{i}", [P, D], F32) for i in lanes]
        x_mid = [sb(f"x_mid{i}", [P, D], F32) for i in lanes]
        h_sb = [sb(f"h_sb{i}", [P, D], F32) for i in lanes]
        hT = [sb(f"hT{i}", [P, KD, P], F32) for i in lanes]
        logit = [sb(f"logit{i}", [P, EXPERTS], F32) for i in lanes]
        logit_nmax = [sb(f"logit_nmax{i}", [P, 1], F32) for i in lanes]
        expo = [sb(f"expo{i}", [P, EXPERTS], F32) for i in lanes]
        expo_sum = [sb(f"expo_sum{i}", [P, 1], F32) for i in lanes]
        expo_inv = [sb(f"expo_inv{i}", [P, 1], F32) for i in lanes]
        score = [sb(f"score{i}", [P, EXPERTS], F32) for i in lanes]
        top = [sb(f"top{i}", [P, TOP_K], F32) for i in lanes]
        struck = [sb(f"struck{i}", [P, EXPERTS], F32) for i in lanes]
        chosen = [sb(f"chosen{i}", [P, P], F32) for i in lanes]
        top_sum = [sb(f"top_sum{i}", [P, 1], F32) for i in lanes]
        chosenT = [sb(f"chosenT{i}", [P, P], F32) for i in lanes]
        y_sb = [sb(f"y_sb{i}", [P, D], F32) for i in lanes]
        y_n = [sb(f"y_n{i}", [P, D], F32) for i in lanes]

        qk_ps = pb("qk_ps")
        v_ps = [pb("v_ps0"), pb("v_ps1")]
        s_ps = pb("s_ps")
        pT_ps = pb("pT_ps")
        z_ps = pb("z_ps")
        o_ps = pb("o_ps")
        aux_ps = [pb("aux_ps"), v_ps[1]]

        x_loaded = [sem(f"x_loaded{b}") for b in range(B)]
        w_loaded = [sem(f"w_loaded{h}") for h in range(HEADS)]
        small_loaded = sem("small_loaded")
        out_stored = sem("out_stored")
        consts_cleared = sem("consts_cleared")
        consts_ready = sem("consts_ready")
        attn_cleared = sem("attn_cleared")
        w_hi_by_pool = sem("w_hi_by_pool")
        vo_weights_scaled = sem("vo_weights_scaled")
        vo_weights_low = sem("vo_weights_low")
        probs_scaled = sem("probs_scaled")
        mid_ready = sem("mid_ready")
        y_normed = sem("y_normed")
        out_ready = sem("out_ready")
        mix_shift_ready = sem("mix_shift_ready")
        w_hi_by_act = sem("w_hi_by_act")
        vo_weights_high = sem("vo_weights_high")
        x_hi_done = sem("x_hi_done")
        qk_hi_done = sem("qk_hi_done")
        v_hi_done = sem("v_hi_done")
        probs_exped = sem("probs_exped")
        pT_hi_done = sem("pT_hi_done")
        z_hi_done = sem("z_hi_done")
        hT_ready = sem("hT_ready")
        expo_ready = sem("expo_ready")
        chosenT_ready = sem("chosenT_ready")
        qk_weights_split = sem("qk_weights_split")
        vo_weights_split = sem("vo_weights_split")
        x_normed = sem("x_normed")
        x_split = sem("x_split")
        qk_split = sem("qk_split")
        v_split = sem("v_split")
        max_found = sem("max_found")
        neg_max_ready = sem("neg_max_ready")
        sums_inverted = sem("sums_inverted")
        pT_split = sem("pT_split")
        z_split = sem("z_split")
        attn_added = sem("attn_added")
        attn_normed = sem("attn_normed")
        h_ready = sem("h_ready")
        logit_biased = sem("logit_biased")
        logit_max_found = sem("logit_max_found")
        expo_inverted = sem("expo_inverted")
        score_ready = sem("score_ready")
        top_found = sem("top_found")
        top_struck = sem("top_struck")
        chosen_ready = sem("chosen_ready")
        top_summed = sem("top_summed")
        y_ready = sem("y_ready")
        stats_of = {s: sem(f"stats_{s}") for s in ("x", "attn", "mid", "mix")}
        moments_of = {s: sem(f"moments_{s}") for s in ("x", "attn", "mid", "mix")}
        var_of = {s: sem(f"var_{s}_ready") for s in ("x", "attn", "mid", "mix")}
        rstd_of = {s: sem(f"rstd_{s}_ready") for s in ("x", "attn", "mid", "mix")}
        x_turned = sem("x_turned")
        qk_projected = sem("qk_projected")
        v_projected = sem("v_projected")
        scores_ready = sem("scores_ready")
        probs_turned = sem("probs_turned")
        z_summed = sem("z_summed")
        o_summed = sem("o_summed")
        h_turned = sem("h_turned")
        logits_ready = sem("logits_ready")
        chosen_turned = sem("chosen_turned")
        mix_ready = sem("mix_ready")

        block = ctx.enter_context(nc.Block())

        def all_units(eng, unit):
            for U in (-2, -1):
                unit(U // ITER, U % ITER)
            for t in (0, 1):
                for k in range(ITER):
                    unit(t, k)
            with eng.Fori(2, LAST) as t:
                for k in range(ITER):
                    unit(t, k)
            for k in range(ITER):
                unit(LAST, k)
            unit(LAST + 1, 0)

        def exists(t, k, ahead):
            return not is_int(t) or 0 <= ITER * t + k + ahead < UNITS

        def is_last(t):
            return is_int(t) and t == LAST

        def number(t, k, ahead=0):
            return t * ITER + (k + ahead)

        def pair_number(t, k):
            return t * (ITER // 2) + k // 2

        X_TILE_AT = {2 * i - 3: i for i in range(2, TILES)}

        def moments(dve, who, lane, src, count):
            bn6, mv, _, _ = norm_of[f"{who}{lane}"]
            nc.vector.bn_stats(bn6[:, :], src).then_inc(stats_of[who], 1)
            n = in_register(dve, count)
            dve.wait_ge(x_loaded[0], 16)
            dve.wait_ge(stats_of[who], n)
            nc.vector.bn_aggr(mv[:, :], bn6[:, :]).then_inc(moments_of[who], 1)

        def inverse_deviation(pool, who, lane, eps, scale, count):
            _, mv, var, rstd = norm_of[f"{who}{lane}"]
            n = in_register(pool, count)
            pool.wait_ge(consts_ready, 2)
            pool.wait_ge(moments_of[who], n)
            nc.gpsimd.tensor_scalar(var[:, :], mv[:, 1:2], eps, scale, ALU.add, ALU.mult).then_inc(var_of[who], 1)
            pool.wait_ge(var_of[who], count)
            nc.gpsimd.tensor_tensor(rstd[:, :], var[:, :], minus_half[:, :], ALU.pow).then_inc(rstd_of[who], 1)

        def normalised(dve, who, lane, dst, src, count, done):
            _, mv, _, rstd = norm_of[f"{who}{lane}"]
            dve.wait_ge(rstd_of[who], count)
            nc.vector.tensor_scalar(dst, src, mv[:, 0:1], rstd[:, 0:1], ALU.subtract, ALU.mult).then_inc(done, 1)

        @block.sync
        def _(sp):
            sp.dma_start(x_sb[:, 0:2, :], x_dram[:, 0:2, :]).then_inc(x_loaded[0], 16)
            for h in range(HEADS):
                if h >= STAGE:
                    sp.wait_ge(qk_weights_split, h - STAGE + 1)
                    if h - STAGE < EARLY:
                        sp.wait_ge(vo_weights_split, h - STAGE + 1)
                    else:
                        sp.wait_ge(vo_weights_low, h - STAGE + 1 - EARLY)
                sp.dma_start(w_raw[:, h % STAGE, :], weights[h]).then_inc(w_loaded[h], 16)
                if 1 <= h < B:
                    sp.dma_start(x_sb[:, 2 * h:2 * h + 2, :], x_dram[:, 2 * h:2 * h + 2, :]).then_inc(x_loaded[h], 16)
                if h == B:
                    sp.dma_start(rw_sb[:, :, :], router_w).then_inc(small_loaded, 16)
                    sp.dma_start(rb_sb[:, :], router_b).then_inc(small_loaded, 16)
                    sp.dma_start(eb_sb[:, :], expert_b).then_inc(small_loaded, 16)
            with sp.Fori(0, TILES) as e:
                sp.wait_ge(out_ready, e + 1)
                sp.dma_start(out_dram[:, bass.ds(e, 1), :], out_sb[:, bass.ds(e, 1), :]).then_inc(out_stored, 16)
            sp.wait_ge(out_stored, 16 * TILES)

        @block.gpsimd
        def _(pool):
            nc.gpsimd.memset(ident[:, :], 0.0).then_inc(consts_cleared, 1)
            nc.gpsimd.memset(minus_half[:, :], -0.5).then_inc(consts_ready, 1)
            pool.wait_ge(consts_cleared, 1)
            nc.gpsimd.affine_select(out=ident[:, :], in_=ident[:, :], compare_op=ALU.not_equal, fill=1.0, base=0,
                                    pattern=[[-1, P]], channel_multiplier=1).then_inc(consts_ready, 1)
            pool.wait_ge(consts_ready, 1)

            def token_rstd(i):
                inverse_deviation(pool, "x", i % 2, EPS, X_SCALE ** -2, i + 1)

            token_rstd(0)
            token_rstd(1)
            nc.gpsimd.memset(ident_b[:, :], 0.0).then_inc(consts_cleared, 1)
            nc.gpsimd.memset(mask_b[:, :, :], 0.0).then_inc(consts_cleared, 1)
            pool.wait_ge(consts_cleared, 3)
            nc.gpsimd.affine_select(out=ident_b[:, :], in_=ident_b[:, :], compare_op=ALU.not_equal, fill=1.0, base=0,
                                    pattern=[[-1, P]], channel_multiplier=1).then_inc(consts_ready, 1)
            nc.gpsimd.affine_select(out=mask_b[:, :, :], in_=mask_b[:, :, :], compare_op=ALU.is_ge, fill=MASK, base=0,
                                    pattern=[[0, 2], [-1, P]], channel_multiplier=1).then_inc(consts_ready, 1)
            nc.gpsimd.memset(attn[:, :, :], 0.0).then_inc(attn_cleared, 1)
            for lane in lanes:
                nc.gpsimd.memset(chosen[lane][:, :], 0.0).then_inc(attn_cleared, 1)

            def finish(lane, e, step):
                if step == 0:
                    inverse_deviation(pool, "attn", lane, EPS * A_SCALE ** 2, 1.0, e + 1)
                if step == 1:
                    pool.wait_ge(attn_normed, e + 1)
                    nc.gpsimd.tensor_tensor(x_mid[lane][:, :], attn_n[lane][:, :], x_sb[:, e, :],
                                            ALU.add).then_inc(mid_ready, 1)
                if step == 2:
                    inverse_deviation(pool, "mid", lane, EPS, 1.0, e + 1)
                if step == 3:
                    inverse_deviation(pool, "mix", lane, EPS, 1.0, e + 1)
                if step == 4:
                    _, mv, _, rstd = norm_of[f"mix{lane}"]
                    n = in_register(pool, e + 1)
                    pool.wait_ge(consts_ready, 2)
                    pool.wait_ge(rstd_of["mix"], n)
                    nc.gpsimd.tensor_scalar(mix_shift[:, :], mv[:, 0:1], rstd[:, 0:1], -1.0,
                                            ALU.mult, ALU.mult).then_inc(mix_shift_ready, 1)
                    n = in_register(pool, e + 1)
                    pool.wait_ge(consts_ready, 2)
                    pool.wait_ge(mix_shift_ready, n)
                    nc.gpsimd.tensor_scalar(y_n[lane][:, :], y_sb[lane][:, :], rstd[:, 0:1], mix_shift[:, 0:1],
                                            ALU.mult, ALU.add).then_inc(y_normed, 1)
                    pool.wait_ge(y_normed, e + 1)
                    nc.gpsimd.tensor_tensor(out_sb[:, e, :], y_n[lane][:, :], x_mid[lane][:, :],
                                            ALU.add).then_inc(out_ready, 1)

            def unit(t, k):
                U = number(t, k)
                if is_int(t) and EARLY <= U + 6 < HEADS:
                    h = U + 6
                    pool.wait_ge(w_loaded[h], 16)
                    nc.gpsimd.tensor_scalar(w_raw[:, h % STAGE, VW:WCOLS], w_raw[:, h % STAGE, VW:WCOLS], W_SCALE,
                                            1.0, ALU.mult, ALU.mult).then_inc(vo_weights_scaled, 1)
                    nc.gpsimd.tensor_scalar(w_hi[:, h, 0:VW], w_raw[:, h % STAGE, 0:VW], W_SCALE, 1.0,
                                            ALU.mult, ALU.mult).then_inc(w_hi_by_pool, 1)
                if exists(t, k, 1):
                    n = in_register(pool, U + 2)
                    pool.wait_ge(consts_ready, 2)
                    pool.wait_ge(sums_inverted, n)
                    s = (k + 1) % 2
                    nc.gpsimd.tensor_scalar(probs[:, s, 0:P], probs[:, s, 0:P], inv_sum[:, s, 0:1], P_SCALE,
                                            ALU.mult, ALU.mult)
                    nc.gpsimd.tensor_scalar(probs[:, s, P:3 * P], probs[:, s, P:3 * P], inv_sum[:, s, 1:2], P_SCALE,
                                            ALU.mult, ALU.mult).then_inc(probs_scaled, 1)
                if is_int(t) and EARLY <= U + 4 < HEADS:
                    h = U + 4
                    pool.wait_ge(vo_weights_high, h + 1 - EARLY)
                    nc.gpsimd.tensor_tensor(w_lo[:, h, VW:WCOLS], w_raw[:, h % STAGE, VW:WCOLS],
                                            w_hi[:, h, VW:WCOLS], ALU.subtract).then_inc(vo_weights_low, 1)
                if is_int(t) and U in X_TILE_AT:
                    token_rstd(X_TILE_AT[U])
                if not is_int(t) or 2 <= t <= LAST:
                    for at, step in ((1, 0), (1, 1), (2, 2), (7, 3), (7, 4)):
                        if k == at:
                            finish(0, t - 2, step)

            all_units(pool, unit)
            for step in (0, 2, 3):
                for lane in lanes:
                    finish(lane, TILES - 2 + lane, step)

        @block.scalar
        def _(act):
            def weights_high(h, first, end):
                act.wait_ge(w_loaded[h], 16)
                nc.scalar.activation(w_hi[:, h, first:end], w_raw[:, h, first:end], ACT.Copy,
                                     scale=W_SCALE).then_inc(w_hi_by_act, 1)

            def tokens_high(i):
                act.wait_ge(x_turned, i + 1)
                nc.scalar.activation(xT_hi[:, :, i * P:(i + 1) * P],
                                     aux_ps[i == 1][:, 0:D].rearrange("p (c n) -> p c n", c=KD),
                                     ACT.Copy).then_inc(x_hi_done, 1)

            def finish(lane, e, step):
                if step == 0:
                    act.wait_ge(h_turned, e + 1)
                    nc.scalar.activation(hT[lane][:, :, :], aux_ps[lane][:, 0:D].rearrange("p (c n) -> p c n", c=KD),
                                         ACT.Copy).then_inc(hT_ready, 1)
                if step == 1:
                    act.wait_ge(logit_max_found, e + 1)
                    nc.scalar.activation(expo[lane][:, :], logit[lane][:, :], ACT.Exp, bias=logit_nmax[lane][:, :],
                                         accum_out=expo_sum[lane][:, :]).then_inc(expo_ready, 1)
                if step == 2:
                    act.wait_ge(chosen_turned, e + 1)
                    nc.scalar.activation(chosenT[lane][:, :], aux_ps[lane][:, 320:320 + P],
                                         ACT.Copy).then_inc(chosenT_ready, 1)

            def unit(t, k):
                U = number(t, k)
                in_finish = not is_int(t) or 2 <= t <= LAST
                if exists(t, k, -1):
                    act.wait_ge(z_summed, U)
                    nc.scalar.activation(z_hi[:, (k + 1) % 2, :], z_ps[:, 0:SEQ], ACT.Copy,
                                         scale=Z_DOWN).then_inc(z_hi_done, 1)
                if in_finish and k == 4:
                    finish(0, t - 2, 0)
                if in_finish and k == 7 and not is_last(t):
                    finish(0, t - 2, 2)
                if exists(t, k, 0):
                    act.wait_ge(probs_turned, U + 1)
                    nc.scalar.activation(pT_hi[:, k % 2, :], pT_ps[:, 0:3 * P], ACT.Copy).then_inc(pT_hi_done, 1)
                if k == 7 and is_last(t):
                    finish(0, t - 2, 2)
                if exists(t, k, 1):
                    act.wait_ge(neg_max_ready, U + 2)
                    s = (k + 1) % 2
                    nc.scalar.activation(probs[:, s, 0:P], s_ps[:, 0:P], ACT.Exp, bias=neg_max[:, s, 0:1],
                                         scale=S_SCALE, accum_out=row_sum[:, s, 0:1])
                    nc.scalar.activation(probs[:, s, P:3 * P], s_ps[:, P:3 * P], ACT.Exp, bias=neg_max[:, s, 1:2],
                                         scale=S_SCALE, accum_out=row_sum[:, s, 1:2]).then_inc(probs_exped, 1)
                if exists(t, k, 2):
                    act.wait_ge(qk_projected, U + 3)
                    nc.scalar.activation(qk_hi[:, k % 2, :], qk_ps[:, :], ACT.Copy,
                                         scale=QKV_DOWN).then_inc(qk_hi_done, 1)
                if in_finish and k == 5:
                    finish(0, t - 2, 1)
                if is_int(t) and U - 3 in X_TILE_AT:
                    tokens_high(X_TILE_AT[U - 3])
                if k % 2 and exists(t, k, 1):
                    act.wait_ge(v_projected, pair_number(t, k) + 2)
                    nc.scalar.activation(v_hi[:, (k // 2 + 1) % 2, :, :, :],
                                         v_ps[(k // 2 + 1) % 2][:, :].rearrange("p (m h n) -> p m h n", m=2, h=2),
                                         ACT.Copy,
                                         scale=QKV_DOWN).then_inc(v_hi_done, 1)
                if is_int(t) and U < 0:
                    weights_high(U + 4, 0, VW)
                    weights_high(U + 4, VW, WCOLS)
                if is_int(t) and EARLY <= U + 5 < HEADS:
                    h = U + 5
                    act.wait_ge(vo_weights_scaled, h + 1 - EARLY)
                    nc.scalar.activation(w_hi[:, h, VW:WCOLS], w_raw[:, h % STAGE, VW:WCOLS],
                                         ACT.Copy).then_inc(vo_weights_high, 1)

            weights_high(0, 0, VW)
            weights_high(1, 0, VW)
            tokens_high(0)
            tokens_high(1)
            weights_high(0, VW, WCOLS)
            weights_high(1, VW, WCOLS)
            all_units(act, unit)
            for step in range(3):
                for lane in lanes:
                    finish(lane, TILES - 2 + lane, step)

        @block.vector
        def _(dve):
            def weights_low(h, first, end, high_done, count, split):
                dve.wait_ge(high_done, count)
                nc.vector.scalar_tensor_tensor(out=w_lo[:, h, first:end], in0=w_raw[:, h % STAGE, first:end],
                                               scalar=W_SCALE, in1=w_hi[:, h, first:end], op0=ALU.mult,
                                               op1=ALU.subtract).then_inc(split, 1)

            def token_moments(i):
                dve.wait_ge(x_loaded[i // 2], 16)
                moments(dve, "x", i % 2, x_sb[:, i, :], i + 1)

            def token_normalise(i):
                normalised(dve, "x", i % 2, xn[:, i % 2, :], x_sb[:, i, :], i + 1, x_normed)

            def tokens_low(i):
                dve.wait_ge(x_hi_done, i + 1)
                nc.vector.scalar_tensor_tensor(out=xT_lo[:, :, i * P:(i + 1) * P],
                                               in0=aux_ps[i == 1][:, 0:D].rearrange("p (c n) -> p c n", c=KD),
                                               scalar=1.0, in1=xT_hi[:, :, i * P:(i + 1) * P],
                                               op0=ALU.mult, op1=ALU.subtract).then_inc(x_split, 1)

            def add_attention(t):
                dve.wait_ge(o_summed, t)
                first = (t - 1) // 2 * 2
                tiles = attn[:, bass.ds(first, 2), :]
                nc.vector.tensor_tensor(tiles, o_ps[:, :].rearrange("p (a d) -> p a d", a=2), tiles,
                                        ALU.add).then_inc(attn_added, 1)

            def finish(lane, e, step):
                if step == 0:
                    dve.wait_ge(attn_added, e + 2 if not is_int(e) else min(e + 2, LAST + 1))
                    moments(dve, "attn", lane, attn[:, e, :], e + 1)
                if step == 1:
                    normalised(dve, "attn", lane, attn_n[lane][:, :], attn[:, e, :], e + 1, attn_normed)
                if step == 2:
                    dve.wait_ge(mid_ready, e + 1)
                    moments(dve, "mid", lane, x_mid[lane][:, :], e + 1)
                if step == 3:
                    normalised(dve, "mid", lane, h_sb[lane][:, :], x_mid[lane][:, :], e + 1, h_ready)
                if step == 4:
                    dve.wait_ge(small_loaded, 16 * 3)
                    dve.wait_ge(logits_ready, e + 1)
                    nc.vector.tensor_tensor(logit[lane][:, :], aux_ps[lane][:, D:D + EXPERTS], rb_sb[:, :],
                                            ALU.add).then_inc(logit_biased, 1)
                    dve.wait_ge(logit_biased, e + 1)
                    nc.vector.tensor_reduce(logit_nmax[lane][:, :], logit[lane][:, :], AX, ALU.max,
                                            negate=True).then_inc(logit_max_found, 1)
                if step == 5:
                    dve.wait_ge(expo_ready, e + 1)
                    nc.vector.reciprocal(expo_inv[lane][:, :], expo_sum[lane][:, :]).then_inc(expo_inverted, 1)
                    dve.wait_ge(expo_inverted, e + 1)
                    nc.vector.tensor_scalar(score[lane][:, :], expo[lane][:, :], expo_inv[lane][:, 0:1], None,
                                            ALU.mult).then_inc(score_ready, 1)
                if step == 6:
                    n = in_register(dve, e + 1)
                    dve.wait_ge(x_loaded[0], 16)
                    dve.wait_ge(score_ready, n)
                    nc.vector.max(top[lane][:, :], score[lane][:, :]).then_inc(top_found, 1)
                    n = in_register(dve, e + 1)
                    dve.wait_ge(x_loaded[0], 16)
                    dve.wait_ge(top_found, n)
                    nc.vector.match_replace(struck[lane][:, :], top[lane][:, :], score[lane][:, :],
                                            -1.0).then_inc(top_struck, 1)
                    nc.vector.reduce_sum(top_sum[lane][:, :], top[lane][:, :], AX).then_inc(top_summed, 1)
                    dve.wait_ge(top_struck, e + 1)
                    nc.vector.scalar_tensor_tensor(out=chosen[lane][:, 0:EXPERTS], in0=struck[lane][:, :], scalar=0.0,
                                                   in1=score[lane][:, :], op0=ALU.is_lt,
                                                   op1=ALU.mult).then_inc(chosen_ready, 1)
                if step == 7:
                    dve.wait_ge(mix_ready, e + 1)
                    dve.wait_ge(top_summed, e + 1)
                    nc.vector.scalar_tensor_tensor(out=y_sb[lane][:, :], in0=h_sb[lane][:, :],
                                                   scalar=top_sum[lane][:, 0:1], in1=aux_ps[lane][:, 0:D],
                                                   op0=ALU.mult, op1=ALU.add).then_inc(y_ready, 1)
                if step == 8:
                    dve.wait_ge(y_ready, e + 1)
                    moments(dve, "mix", lane, y_sb[lane][:, :], e + 1)
                if step == 9:
                    normalised(dve, "mix", lane, y_n[lane][:, :], y_sb[lane][:, :], e + 1, y_normed)
                    dve.wait_ge(y_normed, e + 1)
                    nc.vector.tensor_tensor(out_sb[:, e, :], y_n[lane][:, :], x_mid[lane][:, :],
                                            ALU.add).then_inc(out_ready, 1)

            def v_low(G, slot):
                dve.wait_ge(v_hi_done, G + 1)
                nc.vector.scalar_tensor_tensor(out=v_lo[:, slot, :, :, :].rearrange("p m h n -> p (m h n)"),
                                               in0=v_ps[slot][:, :], scalar=QKV_DOWN,
                                               in1=v_hi[:, slot, :, :, :].rearrange("p m h n -> p (m h n)"),
                                               op0=ALU.mult, op1=ALU.subtract).then_inc(v_split, 1)

            def unit(t, k):
                U = number(t, k)
                in_finish = not is_int(t) or 2 <= t <= LAST
                if exists(t, k, -1):
                    dve.wait_ge(z_hi_done, U)
                    nc.vector.scalar_tensor_tensor(out=z_lo[:, (k + 1) % 2, :], in0=z_ps[:, 0:SEQ], scalar=Z_DOWN,
                                                   in1=z_hi[:, (k + 1) % 2, :], op0=ALU.mult,
                                                   op1=ALU.subtract).then_inc(z_split, 1)
                if exists(t, k, 1):
                    s = (k + 1) % 2
                    dve.wait_ge(scores_ready, U + 2)
                    nc.vector.tensor_reduce(row_max[:, s, 0:1], s_ps[:, 0:P], AX, ALU.max)
                    nc.vector.tensor_reduce(row_max[:, s, 1:2], s_ps[:, P:3 * P], AX, ALU.max).then_inc(max_found, 1)
                    dve.wait_ge(max_found, U + 2)
                    nc.vector.tensor_scalar(neg_max[:, s, :], row_max[:, s, :], -S_SCALE, None,
                                            ALU.mult).then_inc(neg_max_ready, 1)
                if exists(t, k, 0):
                    dve.wait_ge(pT_hi_done, U + 1)
                    nc.vector.scalar_tensor_tensor(out=pT_lo[:, k % 2, :], in0=pT_ps[:, 0:3 * P], scalar=1.0,
                                                   in1=pT_hi[:, k % 2, :], op0=ALU.mult,
                                                   op1=ALU.subtract).then_inc(pT_split, 1)
                if is_int(t) and U - 2 in X_TILE_AT:
                    token_normalise(X_TILE_AT[U - 2])
                if k % 2 == 0 and exists(t, k, 0):
                    v_low(pair_number(t, k), k // 2 % 2)
                if is_int(t) and 4 <= U + 4 < HEADS:
                    weights_low(U + 4, 0, VW, w_hi_by_pool, U + 1, qk_weights_split)
                if in_finish:
                    for at, step in ((1, 0), (3, 3), (5, 4)) + (() if is_last(t) else ((6, 6), (7, 7))):
                        if k == at:
                            finish(0, t - 2, step)
                if exists(t, k, 1):
                    dve.wait_ge(probs_exped, U + 2)
                    nc.vector.reciprocal(inv_sum[:, s, :], row_sum[:, s, :]).then_inc(sums_inverted, 1)
                if exists(t, k, 2):
                    dve.wait_ge(qk_hi_done, U + 3)
                    nc.vector.scalar_tensor_tensor(out=qk_lo[:, k % 2, :], in0=qk_ps[:, :], scalar=QKV_DOWN,
                                                   in1=qk_hi[:, k % 2, :], op0=ALU.mult,
                                                   op1=ALU.subtract).then_inc(qk_split, 1)
                if is_int(t) and U < 0:
                    weights_low(U + 4, 0, VW, w_hi_by_act, 2 * U + 9, qk_weights_split)
                    weights_low(U + 4, VW, WCOLS, w_hi_by_act, 2 * U + 10, vo_weights_split)
                if is_int(t):
                    if U - 3 in X_TILE_AT:
                        tokens_low(X_TILE_AT[U - 3])
                    if U in X_TILE_AT:
                        token_moments(X_TILE_AT[U])
                if k == 0 and not (is_int(t) and t < 1):
                    if is_int(t) and t == 1:
                        dve.wait_ge(attn_cleared, 3)
                    add_attention(t)
                if in_finish:
                    for at, step in ((1, 1), (2, 2), (5, 5)) + (((6, 6), (7, 7)) if is_last(t) else ()) + ((7, 8),):
                        if k == at:
                            finish(0, t - 2, step)

            token_moments(0)
            token_moments(1)
            token_normalise(0)
            weights_low(0, 0, VW, w_hi_by_act, 1, qk_weights_split)
            token_normalise(1)
            weights_low(1, 0, VW, w_hi_by_act, 2, qk_weights_split)
            tokens_low(0)
            tokens_low(1)
            weights_low(0, VW, WCOLS, w_hi_by_act, 3, vo_weights_split)
            weights_low(1, VW, WCOLS, w_hi_by_act, 4, vo_weights_split)
            all_units(dve, unit)
            for step in range(10):
                for lane in lanes:
                    finish(lane, TILES - 2 + lane, step)
                    if step == 1:
                        dve.wait_ge(attn_normed, TILES - 1 + lane)
                        nc.vector.tensor_tensor(x_mid[lane][:, :], attn_n[lane][:, :], x_sb[:, TILES - 2 + lane, :],
                                                ALU.add).then_inc(mid_ready, 1)

        @block.tensor
        def _(pe):
            SPLIT = ((0, 0), (0, 1), (1, 0))
            SPLIT_CHUNKS = [(0, j, c) for c in range(KD) for j in (0, 1)] + [(1, 0, c) for c in range(KD)]
            w = (w_hi, w_lo)
            xT = (xT_hi, xT_lo)
            qk = (qk_hi, qk_lo)
            v = (v_hi, v_lo)
            pT = (pT_hi, pT_lo)
            z = (z_hi, z_lo)

            def place(t, k, ahead, half, batch, next_half, next_batch):
                if is_int(t):
                    return (ITER * t + k + ahead) % HEADS, (ITER * t + k + ahead) // HEADS
                if k + ahead < 0:
                    return next_half * ITER + (k + ahead + ITER), None
                if k + ahead < ITER:
                    return half * ITER + (k + ahead), batch
                return next_half * ITER + (k + ahead - ITER), next_batch

            def tokens_turn(i):
                pe.wait_ge(x_normed, i + 1)
                for c in range(KD):
                    last = nc.tensor.transpose(aux_ps[i == 1][:, c * P:(c + 1) * P], xn[:, i % 2, c * P:(c + 1) * P],
                                               ident[:, :])
                last.then_inc(x_turned, 1)

            def finish(lane, e, step):
                if step == 0:
                    pe.wait_ge(h_ready, e + 1)
                    for c in range(KD):
                        last = nc.tensor.transpose(aux_ps[lane][:, c * P:(c + 1) * P],
                                                   h_sb[lane][:, c * P:(c + 1) * P], ident[:, :])
                    last.then_inc(h_turned, 1)
                if step == 1:
                    pe.wait_ge(hT_ready, e + 1)
                    for c in range(KD):
                        last = nc.tensor.matmul(aux_ps[lane][:, D:D + EXPERTS], hT[lane][:, c, :], rw_sb[:, c, :],
                                                start=(c == 0), stop=(c == KD - 1))
                    last.then_inc(logits_ready, 1)
                if step == 2:
                    pe.wait_ge(chosen_ready, e + 1)
                    nc.tensor.transpose(aux_ps[lane][:, 320:320 + P], chosen[lane][:, :],
                                        ident[:, :]).then_inc(chosen_turned, 1)
                if step == 3:
                    pe.wait_ge(chosenT_ready, e + 1)
                    nc.tensor.matmul(aux_ps[lane][:, 0:D], chosenT[lane][0:EXPERTS, :], eb_sb[:, :],
                                     start=True, stop=True).then_inc(mix_ready, 1)

            def unit(t, k):
                U = number(t, k)
                if is_int(t):
                    half = batch = next_half = next_batch = None
                else:
                    half, batch, next_half, next_batch = regs
                where = (half, batch, next_half, next_batch)

                if exists(t, k, 1):
                    pe.wait_ge(qk_split, U + 2)
                    if positive(U + 1):
                        pe.wait_ge(probs_exped, U + 1)
                    s = (k + 1) % 2
                    diagonals = s_ps[:, :].rearrange("p (a b) -> p a b", b=2 * P)[:, :, 0:P]
                    nc.tensor.matmul(diagonals, ident_b[:, :], mask_b[:, :, :], start=True, stop=False,
                                     skip_group_check=True)
                    for i, j in SPLIT:
                        nc.tensor.matmul(s_ps[:, 0:P], qk[i][:, s, 0:P], qk[j][:, s, SEQ:SEQ + P],
                                         start=False, stop=(i == 1), skip_group_check=True)
                    for i, j in SPLIT:
                        last = nc.tensor.matmul(s_ps[:, P:3 * P], qk[i][:, s, P:2 * P], qk[j][:, s, SEQ:2 * SEQ],
                                                start=False, stop=(i == 1), skip_group_check=True)
                    last.then_inc(scores_ready, 1)
                if exists(t, k, 0):
                    pe.wait_ge(probs_scaled, U + 1)
                    if positive(U):
                        pe.wait_ge(pT_split, U)
                    for n in range(3):
                        last = nc.tensor.transpose(pT_ps[:, n * P:(n + 1) * P], probs[:, k % 2, n * P:(n + 1) * P],
                                                   ident[:, :])
                    last.then_inc(probs_turned, 1)
                if not is_int(t) or 2 <= t <= LAST:
                    if k == 7:
                        finish(0, t - 2, 2 if is_last(t) else 3)
                if exists(t, k, 2):
                    h, b = place(t, k, 2, *where)
                    if is_int(t):
                        pe.wait_ge(qk_weights_split, min(U + 3, HEADS))
                        pe.wait_ge(x_split, 2 * (b + 1))
                    cols = bass.ds(b * SEQ, SEQ)
                    for part, base in ((0, QW), (1, KW)):
                        for n, (i, j, c) in enumerate(SPLIT_CHUNKS):
                            last = nc.tensor.matmul(qk_ps[:, part * SEQ:(part + 1) * SEQ],
                                                    w[i][:, h, base + c * P:base + (c + 1) * P],
                                                    xT[j][:, c, cols], start=(n == 0), stop=(n == 5))
                    last.then_inc(qk_projected, 1)
                if exists(t, k, -1):
                    pe.wait_ge(z_split, U)
                    if k == 1 and positive(t):
                        pe.wait_ge(attn_added, t)
                    h, _ = place(t, k, -1, *where)
                    s = (k + 1) % 2
                    for a in range(2):
                        for n, (i, j) in enumerate(SPLIT):
                            last = nc.tensor.matmul(o_ps[:, a * D:(a + 1) * D], z[i][:, s, a * P:(a + 1) * P],
                                                    w[j][:, h, OW:OW + D], start=(k == 1 and a == 0 and n == 0),
                                                    stop=(k == 0), skip_group_check=True)
                    if k == 0:
                        last.then_inc(o_summed, 1)
                if exists(t, k, 2 - k % 2):
                    h, b = place(t, k, 2 - k % 2, *where)
                    a = k % 2
                    if a == 0 and positive(pair_number(t, k)):
                        pe.wait_ge(v_split, pair_number(t, k))
                    if is_int(t) and U + 2 < HEADS:
                        if h + 1 < EARLY:
                            pe.wait_ge(vo_weights_split, h + 2)
                        else:
                            pe.wait_ge(vo_weights_low, h + 2 - EARLY)
                    for n, (i, j, c) in enumerate(SPLIT_CHUNKS):
                        last = nc.tensor.matmul(v_ps[(k // 2 + 1) % 2][:, a * 2 * DH:(a + 1) * 2 * DH],
                                                xT[i][:, c, bass.ds(b * SEQ + a * P, P)],
                                                w[j][:, bass.ds(h, 2), VW + c * P:VW + (c + 1) * P],
                                                start=(n == 0), stop=(n == 5))
                    if a == 1:
                        last.then_inc(v_projected, 1)
                if is_int(t) and U - 2 in X_TILE_AT:
                    tokens_turn(X_TILE_AT[U - 2])
                if not is_int(t) or 2 <= t <= LAST:
                    for at, step in ((3, 0), (4, 1)) + (((7, 3),) if is_last(t) else ((6, 2),)):
                        if k == at:
                            finish(0, t - 2, step)
                if exists(t, k, 0):
                    pe.wait_ge(pT_split, U + 1)
                    pe.wait_ge(v_split, pair_number(t, k) + 1)
                    g, hh, s = k // 2 % 2, k % 2, k % 2
                    for n, (i, j) in enumerate(SPLIT):
                        nc.tensor.matmul(z_ps[:, 0:SEQ], v[i][:, g, 0, hh, :], pT[j][:, s, 0:SEQ],
                                         start=(n == 0), stop=False, skip_group_check=True)
                    for n, (i, j) in enumerate(SPLIT):
                        last = nc.tensor.matmul(z_ps[:, P:SEQ], v[i][:, g, 1, hh, :], pT[j][:, s, SEQ:3 * P],
                                                start=False, stop=(n == 2), skip_group_check=True)
                    last.then_inc(z_summed, 1)

            pe.wait_ge(consts_ready, 2)
            tokens_turn(0)
            tokens_turn(1)
            pe.wait_ge(consts_ready, 4)
            regs = None
            for U in (-2, -1):
                unit(-1, U % ITER)
            for t in (0, 1):
                for k in range(ITER):
                    unit(t, k)
            with pe.Fori(2, LAST) as t:
                regs = (pe.snap(t % 2), pe.snap(t // 2), pe.snap((t + 1) % 2), pe.snap((t + 1) // 2))
                for k in range(ITER):
                    unit(t, k)
            for k in range(ITER):
                unit(LAST, k)
            unit(LAST + 1, 0)
            for step in range(4):
                for lane in lanes:
                    finish(lane, TILES - 2 + lane, step)


def kernel(**inputs):
    import numpy as _np
    import concourse.bacc as _bacc
    from concourse.bass_utils import run_bass_kernel_spmd as _run

    x = _np.ascontiguousarray(inputs["L0_attn_x"]).reshape(B * SEQ, D)

    def head_rows(w):
        w = _np.asarray(w).transpose(0, 2, 1).reshape(HEADS, KD, P, DH)
        return w.transpose(0, 2, 1, 3).reshape(HEADS, P, KD * DH)

    w_o = _np.asarray(inputs["L0_attn_W_O"]).transpose(0, 2, 1)
    weights = _np.ascontiguousarray(_np.concatenate(
        [head_rows(inputs["L0_attn_W_Q"]), head_rows(inputs["L0_attn_W_K"]), head_rows(inputs["L0_attn_W_V"]), w_o],
        axis=2))
    router_w = _np.ascontiguousarray(
        _np.asarray(inputs["L0_ffn_router_weight"]).T.reshape(KD, P, EXPERTS).transpose(1, 0, 2))
    router_b = _np.ascontiguousarray(_np.broadcast_to(_np.asarray(inputs["L0_ffn_router_bias"]), (P, EXPERTS)))
    expert_b = _np.ascontiguousarray(inputs["L0_ffn_expert_bias"])

    nc = _bacc.Bacc("TRN2", target_bir_lowering=False, num_devices=1)
    arrays, args = {}, []
    for name, a in (("x", x), ("weights", weights), ("router_w", router_w), ("router_b", router_b),
                    ("expert_b", expert_b)):
        arrays[f"in_{name}_dram"] = a
        args.append(nc.dram_tensor(f"in_{name}_dram", a.shape, F32, kind="ExternalInput").ap())
    args.append(nc.dram_tensor("out_0_dram", (B * SEQ, D), F32, kind="ExternalOutput").ap())
    layer_kernel(nc, *args)
    r = _run(nc, [arrays], core_ids=[0])
    return r.results[0]["out_0_dram"].reshape(B, SEQ, D)
```

```python
from contextlib import ExitStack

import concourse.bass as bass
from concourse import mybir

F32 = mybir.dt.float32
F16 = mybir.dt.float16
ALU = mybir.AluOpType
ACT = mybir.ActivationFunctionType
AX = mybir.AxisListType.X

P = 128
B, SEQ, D = 4, 256, 256
HEADS, DH = 16, 128
EXPERTS, TOP_K = 64, 8
KD = D // P
TILES = B * SEQ // P
UNITS = B * HEADS
ITER = 8
LAST = UNITS // ITER - 1
WCOLS = 3 * D + D
QW, KW, VW, OW = 0, D, 2 * D, 3 * D
STAGE = 8
EARLY = 4
EPS = 1e-5
NEG = -1.0e9

X_SCALE = 8.0
W_SCALE = 64.0
QKV_DOWN = 0.125
QKV_SCALE = X_SCALE * W_SCALE * QKV_DOWN
P_SCALE = 16384.0
Z_DOWN = 1.0 / 16384.0
A_SCALE = QKV_SCALE * W_SCALE
S_SCALE = float(DH) ** -0.5 / QKV_SCALE ** 2
MASK = NEG / S_SCALE
HUGE = 3.0e38
STRUCK = -3.0e38


def is_int(v):
    return isinstance(v, int)


def positive(count):
    return not is_int(count) or count > 0


def in_register(eng, count):
    return count if is_int(count) else eng.to_reg(count)


def layer_kernel(nc, x, weights, router_w, router_b, expert_b, out):
    x_dram = x.rearrange("(t p) d -> p t d", p=P)
    out_dram = out.rearrange("(t p) d -> p t d", p=P)

    with ExitStack() as ctx:
        def sb(name, shape, dt):
            return ctx.enter_context(nc.sbuf_tensor(name, shape, dt))

        def pb(name, cols=512):
            return ctx.enter_context(nc.psum_tensor(name, [P, cols], F32))

        def sem(name):
            return ctx.enter_context(nc.semaphore(name))

        x_sb = sb("x_sb", [P, TILES, D], F32)
        w_raw = sb("w_raw", [P, STAGE, WCOLS], F32)
        w_hi = sb("w_hi", [P, HEADS, WCOLS], F16)
        w_lo = sb("w_lo", [P, HEADS, WCOLS], F16)
        xT_hi = sb("xT_hi", [P, KD, TILES * P], F16)
        xT_lo = sb("xT_lo", [P, KD, TILES * P], F16)
        xn = sb("xn", [P, 2, D], F32)
        qk_hi = sb("qk_hi", [P, 2, 2 * SEQ], F16)
        qk_lo = sb("qk_lo", [P, 2, 2 * SEQ], F16)
        v_hi = sb("v_hi", [P, 2, 2, 2, DH], F16)
        v_lo = sb("v_lo", [P, 2, 2, 2, DH], F16)
        probs = sb("probs", [P, 2, 3 * P], F32)
        pT_hi = sb("pT_hi", [P, 2, 3 * P], F16)
        pT_lo = sb("pT_lo", [P, 2, 3 * P], F16)
        z_hi = sb("z_hi", [P, 2, SEQ], F16)
        z_lo = sb("z_lo", [P, 2, SEQ], F16)
        neg_scores = sb("neg_scores", [P, 2, 3 * P], F32)
        neg_max = sb("neg_max", [P, 2, 2], F32)
        row_sum = sb("row_sum", [P, 2, 2], F32)
        inv_sum = sb("inv_sum", [P, 2, 2], F32)
        attn = sb("attn", [P, TILES, D], F32)
        out_sb = sb("out_sb", [P, TILES, D], F32)
        ident = sb("ident", [P, P], F32)
        mask = sb("mask", [P, 2 * P], F32)
        minus_half = sb("minus_half", [P, 1], F32)
        rw_sb = sb("rw_sb", [P, KD, EXPERTS], F32)
        rw_mid = sb("rw_mid", [P, KD, EXPERTS], F32)
        averager = sb("averager", [P, P], F32)
        rb_sb = sb("rb_sb", [P, EXPERTS], F32)
        eb_sb = sb("eb_sb", [EXPERTS, D], F32)
        lanes = range(3)
        norm_of = {}
        for who in ["x0", "x1"] + [f"{s}{lane}" for s in ("attn", "mid", "mix") for lane in lanes]:
            norm_of[who] = (sb(f"bn6_{who}", [P, 6], F32), sb(f"mv_{who}", [P, 2], F32),
                            sb(f"var_{who}", [P, 1], F32), sb(f"rstd_{who}", [P, 1], F32))
        mix_shift = sb("mix_shift", [P, 1], F32)
        mix_eps = [sb(f"mix_eps{i}", [P, 1], F32) for i in lanes]
        attn_n = [sb(f"attn_n{i}", [P, D], F32) for i in lanes]
        x_mid = [sb(f"x_mid{i}", [P, D], F32) for i in lanes]
        h_sb = [sb(f"h_sb{i}", [P, D], F32) for i in lanes]
        midT = [sb(f"midT{i}", [P, KD, P], F32) for i in lanes]
        logit = [sb(f"logit{i}", [P, EXPERTS], F32) for i in lanes]
        logit_nmax = [sb(f"logit_nmax{i}", [P, 1], F32) for i in lanes]
        expo = [sb(f"expo{i}", [P, EXPERTS], F32) for i in lanes]
        expo_sum = [sb(f"expo_sum{i}", [P, 1], F32) for i in lanes]
        top = [sb(f"top{i}", [P, TOP_K], F32) for i in lanes]
        struck = [sb(f"struck{i}", [P, EXPERTS], F32) for i in lanes]
        chosen = [sb(f"chosen{i}", [P, P], F32) for i in lanes]
        top_sum = [sb(f"top_sum{i}", [P, 1], F32) for i in lanes]
        chosenT = [sb(f"chosenT{i}", [P, P], F32) for i in lanes]
        y_sb = [sb(f"y_sb{i}", [P, D], F32) for i in lanes]
        y_n = [sb(f"y_n{i}", [P, D], F32) for i in lanes]

        qk_ps = pb("qk_ps")
        v_ps = [pb("v_ps0"), pb("v_ps1")]
        s_ps = pb("s_ps")
        pT_ps = pb("pT_ps")
        z_ps = pb("z_ps")
        o_ps = pb("o_ps")
        aux_ps = [pb("aux_ps"), v_ps[1]]
        last_o = [o_ps, v_ps[0]]
        aux_of_lane = [aux_ps[0], s_ps, aux_ps[1]]

        x_loaded = [sem(f"x_loaded{b}") for b in range(B)]
        x1_loaded = sem("x1_loaded")
        w_loaded = [sem(f"w_loaded{h}") for h in range(HEADS)]
        small_loaded = sem("small_loaded")
        out_stored = sem("out_stored")
        consts_cleared = sem("consts_cleared")
        consts_ready = sem("consts_ready")
        attn_cleared = sem("attn_cleared")
        w_hi_by_pool = sem("w_hi_by_pool")
        vo_weights_scaled = sem("vo_weights_scaled")
        vo_weights_low = sem("vo_weights_low")
        probs_scaled = sem("probs_scaled")
        mid_ready = sem("mid_ready")
        y_normed = sem("y_normed")
        out_ready = sem("out_ready")
        mix_shift_ready = sem("mix_shift_ready")
        mix_eps_ready = sem("mix_eps_ready")
        w_hi_by_act = sem("w_hi_by_act")
        vo_weights_high = sem("vo_weights_high")
        x_hi_done = sem("x_hi_done")
        qk_hi_done = sem("qk_hi_done")
        v_hi_done = sem("v_hi_done")
        probs_exped = sem("probs_exped")
        pT_hi_done = sem("pT_hi_done")
        z_hi_done = sem("z_hi_done")
        midT_ready = sem("midT_ready")
        expo_ready = sem("expo_ready")
        chosenT_ready = sem("chosenT_ready")
        qk_weights_split = sem("qk_weights_split")
        vo_weights_split = sem("vo_weights_split")
        x_normed = sem("x_normed")
        x_split = sem("x_split")
        qk_split = sem("qk_split")
        v_split = sem("v_split")
        neg_max_ready = sem("neg_max_ready")
        sums_inverted = sem("sums_inverted")
        pT_split = sem("pT_split")
        z_split = sem("z_split")
        attn_added = sem("attn_added")
        attn_normed = sem("attn_normed")
        attn_centred = sem("attn_centred")
        y_centred = sem("y_centred")
        h_ready = sem("h_ready")
        logit_biased = sem("logit_biased")
        logit_max_found = sem("logit_max_found")
        top_found = sem("top_found")
        top_struck = sem("top_struck")
        chosen_ready = sem("chosen_ready")
        top_summed = sem("top_summed")
        router_centred = sem("router_centred")
        y_ready = sem("y_ready")
        stats_of = {s: sem(f"stats_{s}") for s in ("x", "attn", "mid", "mix")}
        moments_of = {s: sem(f"moments_{s}") for s in ("x", "attn", "mid", "mix")}
        var_of = {s: sem(f"var_{s}_ready") for s in ("x", "attn", "mid", "mix")}
        rstd_of = {s: sem(f"rstd_{s}_ready") for s in ("x", "attn", "mid", "mix")}
        x_turned = sem("x_turned")
        qk_projected = sem("qk_projected")
        v_projected = sem("v_projected")
        scores_ready = sem("scores_ready")
        probs_turned = sem("probs_turned")
        z_summed = sem("z_summed")
        o_summed = sem("o_summed")
        router_averaged = sem("router_averaged")
        mid_turned = sem("mid_turned")
        logits_ready = sem("logits_ready")
        chosen_turned = sem("chosen_turned")
        mix_ready = sem("mix_ready")

        block = ctx.enter_context(nc.Block())

        def all_units(eng, fill, unit):
            fill()
            for U in range(1, 2 * ITER):
                unit(U // ITER, U % ITER)
            with eng.Fori(2, LAST) as t:
                for k in range(ITER):
                    unit(t, k)
            for k in range(ITER):
                unit(LAST, k)
            unit(LAST + 1, 0)

        def exists(t, k, ahead):
            return not is_int(t) or 0 <= ITER * t + k + ahead < UNITS

        def is_last(t):
            return is_int(t) and t == LAST

        def qk_bank(t, k):
            return z_ps if is_int(t) and number(t, k) == -1 else qk_ps

        def number(t, k, ahead=0):
            return t * ITER + (k + ahead)

        def pair_number(t, k):
            return t * (ITER // 2) + k // 2

        X_TILE_AT = {2 * i - 3: i for i in range(2, TILES)}

        def stats(who, lane, src):
            nc.vector.bn_stats(norm_of[f"{who}{lane}"][0][:, :], src).then_inc(stats_of[who], 1)

        def moments(dve, who, lane, count):
            bn6, mv, _, _ = norm_of[f"{who}{lane}"]
            n = in_register(dve, count)
            dve.wait_ge(x_loaded[0], 16)
            dve.wait_ge(stats_of[who], n)
            nc.vector.bn_aggr(mv[:, :], bn6[:, :]).then_inc(moments_of[who], 1)

        def inverse_deviation(pool, who, lane, eps, scale, count):
            _, mv, var, rstd = norm_of[f"{who}{lane}"]
            n = in_register(pool, count)
            pool.wait_ge(consts_ready, 2)
            if who == "mix":
                pool.wait_ge(mix_eps_ready, n)
            pool.wait_ge(moments_of[who], n)
            nc.gpsimd.tensor_scalar(var[:, :], mv[:, 1:2], eps, scale, ALU.add, ALU.mult).then_inc(var_of[who], 1)
            pool.wait_ge(var_of[who], count)
            nc.gpsimd.tensor_tensor(rstd[:, :], var[:, :], minus_half[:, :], ALU.pow).then_inc(rstd_of[who], 1)

        def normalised(dve, who, lane, dst, src, count, done):
            _, mv, _, rstd = norm_of[f"{who}{lane}"]
            dve.wait_ge(rstd_of[who], count)
            nc.vector.tensor_scalar(dst, src, mv[:, 0:1], rstd[:, 0:1], ALU.subtract, ALU.mult).then_inc(done, 1)

        @block.sync
        def _(sp):
            sp.dma_start(x_sb[:, 0, :], x_dram[:, 0, :]).then_inc(x_loaded[0], 16)
            sp.dma_start(x_sb[:, 1, :], x_dram[:, 1, :]).then_inc(x1_loaded, 16)
            for h in range(HEADS):
                if h >= STAGE:
                    sp.wait_ge(qk_weights_split, h - STAGE + 1)
                    if h - STAGE < EARLY:
                        sp.wait_ge(vo_weights_split, h - STAGE + 1)
                    else:
                        sp.wait_ge(vo_weights_low, h - STAGE + 1 - EARLY)
                sp.dma_start(w_raw[:, h % STAGE, :], weights[h]).then_inc(w_loaded[h], 16)
                b = h - EARLY + 1
                if 1 <= b < B:
                    sp.dma_start(x_sb[:, 2 * b:2 * b + 2, :], x_dram[:, 2 * b:2 * b + 2, :]).then_inc(x_loaded[b], 16)
                if b == B:
                    sp.dma_start(rw_sb[:, :, :], router_w).then_inc(small_loaded, 16)
                    sp.dma_start(rb_sb[:, :], router_b).then_inc(small_loaded, 16)
                    sp.dma_start(eb_sb[:, :], expert_b).then_inc(small_loaded, 16)
            with sp.Fori(0, TILES) as e:
                sp.wait_ge(out_ready, e + 1)
                sp.dma_start(out_dram[:, bass.ds(e, 1), :], out_sb[:, bass.ds(e, 1), :]).then_inc(out_stored, 16)
            sp.wait_ge(out_stored, 16 * TILES)

        @block.gpsimd
        def _(pool):
            nc.gpsimd.memset(ident[:, :], 0.0).then_inc(consts_cleared, 1)
            nc.gpsimd.memset(minus_half[:, :], -0.5).then_inc(consts_ready, 1)
            pool.wait_ge(consts_cleared, 1)
            nc.gpsimd.affine_select(out=ident[:, :], in_=ident[:, :], compare_op=ALU.not_equal, fill=1.0, base=0,
                                    pattern=[[-1, P]], channel_multiplier=1).then_inc(consts_ready, 1)
            pool.wait_ge(consts_ready, 1)

            def token_rstd(i):
                inverse_deviation(pool, "x", i % 2, EPS, X_SCALE ** -2, i + 1)

            token_rstd(0)
            token_rstd(1)
            nc.gpsimd.memset(mask[:, :], 0.0).then_inc(consts_cleared, 1)
            pool.wait_ge(consts_cleared, 2)
            nc.gpsimd.affine_select(out=mask[:, P:2 * P], in_=mask[:, P:2 * P], compare_op=ALU.is_ge, fill=MASK,
                                    base=0, pattern=[[-1, P]], channel_multiplier=1).then_inc(consts_ready, 1)
            nc.gpsimd.memset(averager[:, :], 1.0 / D).then_inc(consts_ready, 1)
            nc.gpsimd.memset(attn[:, :, :], 0.0).then_inc(attn_cleared, 1)
            for lane in lanes:
                nc.gpsimd.memset(chosen[lane][:, :], 0.0).then_inc(attn_cleared, 1)

            def finish(lane, e, step):
                if step == "attn rstd":
                    inverse_deviation(pool, "attn", lane, EPS * A_SCALE ** 2, 1.0, e + 1)
                if step == "residual":
                    pool.wait_ge(attn_normed, e + 1)
                    nc.gpsimd.tensor_tensor(x_mid[lane][:, :], attn_n[lane][:, :], x_sb[:, e, :],
                                            ALU.add).then_inc(mid_ready, 1)
                if step == "mid rstd":
                    inverse_deviation(pool, "mid", lane, EPS, 1.0, e + 1)
                if step == "mix rstd":
                    inverse_deviation(pool, "mix", lane, mix_eps[lane][:, 0:1], 1.0, e + 1)
                if step == "mix eps":
                    n = in_register(pool, e + 1)
                    pool.wait_ge(consts_ready, 2)
                    pool.wait_ge(expo_ready, n)
                    nc.gpsimd.tensor_scalar(mix_eps[lane][:, :], expo_sum[lane][:, :], expo_sum[lane][:, 0:1], EPS,
                                            ALU.mult, ALU.mult).then_inc(mix_eps_ready, 1)
                if step == "output":
                    _, mv, _, rstd = norm_of[f"mix{lane}"]
                    n = in_register(pool, e + 1)
                    pool.wait_ge(consts_ready, 2)
                    pool.wait_ge(rstd_of["mix"], n)
                    nc.gpsimd.tensor_scalar(mix_shift[:, :], mv[:, 0:1], rstd[:, 0:1], -1.0,
                                            ALU.mult, ALU.mult).then_inc(mix_shift_ready, 1)
                    n = in_register(pool, e + 1)
                    pool.wait_ge(consts_ready, 2)
                    pool.wait_ge(mix_shift_ready, n)
                    nc.gpsimd.tensor_scalar(y_n[lane][:, :], y_sb[lane][:, :], rstd[:, 0:1], mix_shift[:, 0:1],
                                            ALU.mult, ALU.add).then_inc(y_normed, 1)
                    pool.wait_ge(y_normed, e + 1)
                    nc.gpsimd.tensor_tensor(out_sb[:, e, :], y_n[lane][:, :], x_mid[lane][:, :],
                                            ALU.add).then_inc(out_ready, 1)

            STEPS = {1: ("attn rstd", "residual"), 2: ("mid rstd",), 6: ("mix eps",), 7: ("mix rstd", "output")}
            LAST_STEPS = {1: ("attn rstd", "residual"), 2: ("mid rstd",), 7: ("mix eps",)}

            def weights(t, k):
                U = number(t, k)
                if is_int(t) and EARLY <= U + 6 < HEADS:
                    h = U + 6
                    pool.wait_ge(w_loaded[h], 16)
                    nc.gpsimd.tensor_scalar(w_raw[:, h % STAGE, VW:WCOLS], w_raw[:, h % STAGE, VW:WCOLS], W_SCALE,
                                            1.0, ALU.mult, ALU.mult).then_inc(vo_weights_scaled, 1)
                    nc.gpsimd.tensor_scalar(w_hi[:, h, 0:VW], w_raw[:, h % STAGE, 0:VW], W_SCALE, 1.0,
                                            ALU.mult, ALU.mult).then_inc(w_hi_by_pool, 1)

            def scale_probs(t, k):
                U = number(t, k)
                if exists(t, k, 1) and not (is_int(t) and U + 1 == UNITS - 1):
                    n = in_register(pool, U + 2)
                    pool.wait_ge(consts_ready, 2)
                    pool.wait_ge(sums_inverted, n)
                    s = (k + 1) % 2
                    nc.gpsimd.tensor_scalar(probs[:, s, 0:P], probs[:, s, 0:P], inv_sum[:, s, 0:1], P_SCALE,
                                            ALU.mult, ALU.mult)
                    nc.gpsimd.tensor_scalar(probs[:, s, P:3 * P], probs[:, s, P:3 * P], inv_sum[:, s, 1:2], P_SCALE,
                                            ALU.mult, ALU.mult).then_inc(probs_scaled, 1)

            def vo_low(t, k):
                U = number(t, k)
                if is_int(t) and EARLY <= U + 4 < HEADS:
                    h = U + 4
                    pool.wait_ge(vo_weights_high, h + 1 - EARLY)
                    nc.gpsimd.tensor_tensor(w_lo[:, h, VW:WCOLS], w_raw[:, h % STAGE, VW:WCOLS],
                                            w_hi[:, h, VW:WCOLS], ALU.subtract).then_inc(vo_weights_low, 1)

            def fill():
                weights(-1, 6)
                scale_probs(-1, 7)
                weights(-1, 7)
                scale_probs(0, 0)
                weights(0, 0)
                vo_low(0, 0)

            def unit(t, k):
                U = number(t, k)
                weights(t, k)
                scale_probs(t, k)
                vo_low(t, k)
                if is_int(t) and U in X_TILE_AT:
                    token_rstd(X_TILE_AT[U])
                if not is_int(t) or 2 <= t <= LAST:
                    for step in (LAST_STEPS if is_last(t) else STEPS).get(k, ()):
                        finish(0, t - 2, step)

            all_units(pool, fill, unit)
            finish(1, TILES - 2, "attn rstd")
            finish(2, TILES - 1, "attn rstd")
            finish(1, TILES - 2, "mid rstd")
            finish(2, TILES - 1, "mid rstd")
            finish(1, TILES - 2, "mix eps")
            finish(2, TILES - 1, "mix eps")
            finish(0, TILES - 3, "mix rstd")
            finish(0, TILES - 3, "output")
            finish(1, TILES - 2, "mix rstd")
            finish(2, TILES - 1, "mix rstd")

        @block.scalar
        def _(act):
            def weights_high(h, first, end):
                act.wait_ge(w_loaded[h], 16)
                nc.scalar.activation(w_hi[:, h, first:end], w_raw[:, h, first:end], ACT.Copy,
                                     scale=W_SCALE).then_inc(w_hi_by_act, 1)

            def tokens_high(i):
                act.wait_ge(x_turned, i + 1)
                nc.scalar.activation(xT_hi[:, :, i * P:(i + 1) * P],
                                     aux_ps[i == 1][:, 0:D].rearrange("p (c n) -> p c n", c=KD),
                                     ACT.Copy).then_inc(x_hi_done, 1)

            def finish(lane, e, step):
                if step == "copy mid":
                    act.wait_ge(mid_turned, e + 1)
                    nc.scalar.activation(midT[lane][:, :, :],
                                         aux_of_lane[lane][:, 0:D].rearrange("p (c n) -> p c n", c=KD),
                                         ACT.Copy).then_inc(midT_ready, 1)
                if step == "exponentials":
                    act.wait_ge(logit_max_found, e + 1)
                    nc.scalar.activation(expo[lane][:, :], logit[lane][:, :], ACT.Exp, bias=logit_nmax[lane][:, :],
                                         accum_out=expo_sum[lane][:, :]).then_inc(expo_ready, 1)
                if step == "copy chosen":
                    act.wait_ge(chosen_turned, e + 1)
                    nc.scalar.activation(chosenT[lane][:, :], aux_of_lane[lane][:, 320:320 + P],
                                         ACT.Copy).then_inc(chosenT_ready, 1)

            def probs_high(t, k):
                U = number(t, k)
                if exists(t, k, 0):
                    act.wait_ge(probs_turned, U + 1)
                    nc.scalar.activation(pT_hi[:, k % 2, :], pT_ps[:, 0:3 * P], ACT.Copy).then_inc(pT_hi_done, 1)

            def exponentials(t, k):
                U = number(t, k)
                if exists(t, k, 1):
                    act.wait_ge(neg_max_ready, U + 2)
                    s = (k + 1) % 2
                    nc.scalar.activation(probs[:, s, 0:P], neg_scores[:, s, 0:P], ACT.Exp, bias=neg_max[:, s, 0:1],
                                         scale=-1.0, accum_out=row_sum[:, s, 0:1])
                    nc.scalar.activation(probs[:, s, P:3 * P], neg_scores[:, s, P:3 * P], ACT.Exp,
                                         bias=neg_max[:, s, 1:2], scale=-1.0,
                                         accum_out=row_sum[:, s, 1:2]).then_inc(probs_exped, 1)

            def queries_keys_high(t, k):
                U = number(t, k)
                if exists(t, k, 2):
                    act.wait_ge(qk_projected, U + 3)
                    nc.scalar.activation(qk_hi[:, k % 2, :], qk_bank(t, k)[:, :], ACT.Copy,
                                         scale=QKV_DOWN).then_inc(qk_hi_done, 1)

            def values_high(t, k):
                if k % 2 and exists(t, k, 1):
                    act.wait_ge(v_projected, pair_number(t, k) + 2)
                    nc.scalar.activation(v_hi[:, (k // 2 + 1) % 2, :, :, :],
                                         v_ps[(k // 2 + 1) % 2][:, :].rearrange("p (m h n) -> p m h n", m=2, h=2),
                                         ACT.Copy,
                                         scale=QKV_DOWN).then_inc(v_hi_done, 1)

            def vo_high(t, k):
                U = number(t, k)
                if is_int(t) and EARLY <= U + 5 < HEADS:
                    h = U + 5
                    act.wait_ge(vo_weights_scaled, h + 1 - EARLY)
                    nc.scalar.activation(w_hi[:, h, VW:WCOLS], w_raw[:, h % STAGE, VW:WCOLS],
                                         ACT.Copy).then_inc(vo_weights_high, 1)

            def fill():
                queries_keys_high(-1, 6)
                weights_high(2, 0, VW)
                weights_high(2, VW, WCOLS)
                queries_keys_high(-1, 7)
                weights_high(3, 0, VW)
                exponentials(-1, 7)
                values_high(-1, 7)
                weights_high(3, VW, WCOLS)
                exponentials(0, 0)
                probs_high(0, 0)
                queries_keys_high(0, 0)
                vo_high(-1, 7)
                vo_high(0, 0)

            def unit(t, k):
                U = number(t, k)
                in_finish = not is_int(t) or 2 <= t <= LAST
                if exists(t, k, -1):
                    act.wait_ge(z_summed, U)
                    nc.scalar.activation(z_hi[:, (k + 1) % 2, :], z_ps[:, 0:SEQ], ACT.Copy,
                                         scale=Z_DOWN).then_inc(z_hi_done, 1)
                if in_finish and k == 4:
                    finish(0, t - 2, "copy mid")
                if in_finish and k == 7 and not is_last(t):
                    finish(0, t - 2, "copy chosen")
                probs_high(t, k)
                if k == 7 and is_last(t):
                    finish(0, t - 2, "copy chosen")
                exponentials(t, k)
                queries_keys_high(t, k)
                if in_finish and k == 5:
                    finish(0, t - 2, "exponentials")
                if is_int(t) and U - 3 in X_TILE_AT:
                    tokens_high(X_TILE_AT[U - 3])
                values_high(t, k)
                vo_high(t, k)

            weights_high(0, 0, VW)
            tokens_high(0)
            tokens_high(1)
            weights_high(1, 0, VW)
            weights_high(0, VW, WCOLS)
            weights_high(1, VW, WCOLS)
            all_units(act, fill, unit)
            for step in ("copy mid", "exponentials", "copy chosen"):
                for lane in (1, 2):
                    finish(lane, TILES - 3 + lane, step)

        @block.vector
        def _(dve):
            def weights_low(h, first, end, high_done, count, split):
                dve.wait_ge(high_done, count)
                nc.vector.scalar_tensor_tensor(out=w_lo[:, h, first:end], in0=w_raw[:, h % STAGE, first:end],
                                               scalar=W_SCALE, in1=w_hi[:, h, first:end], op0=ALU.mult,
                                               op1=ALU.subtract).then_inc(split, 1)

            def token_moments(i):
                dve.wait_ge(x1_loaded if i == 1 else x_loaded[i // 2], 16)
                stats("x", i % 2, x_sb[:, i, :])
                moments(dve, "x", i % 2, i + 1)

            def token_normalise(i):
                normalised(dve, "x", i % 2, xn[:, i % 2, :], x_sb[:, i, :], i + 1, x_normed)

            def tokens_low(i):
                dve.wait_ge(x_hi_done, i + 1)
                nc.vector.scalar_tensor_tensor(out=xT_lo[:, :, i * P:(i + 1) * P],
                                               in0=aux_ps[i == 1][:, 0:D].rearrange("p (c n) -> p c n", c=KD),
                                               scalar=1.0, in1=xT_hi[:, :, i * P:(i + 1) * P],
                                               op0=ALU.mult, op1=ALU.subtract).then_inc(x_split, 1)

            def add_attention(t):
                dve.wait_ge(o_summed, t)
                first = (t - 1) // 2 * 2
                tiles = attn[:, bass.ds(first, 2), :]
                nc.vector.tensor_tensor(tiles, o_ps[:, :].rearrange("p (a d) -> p a d", a=2), tiles,
                                        ALU.add).then_inc(attn_added, 1)

            def finish(lane, e, step):
                if step == "last head":
                    dve.wait_ge(o_summed, e + 3)
                    nc.vector.tensor_tensor(attn[:, e, :], last_o[lane - 1][:, 0:D], attn[:, e, :],
                                            ALU.add).then_inc(attn_added, 1)
                if step == "attn stats":
                    dve.wait_ge(attn_added, e + 2 if lane == 0 else e + 3)
                    stats("attn", lane, attn[:, e, :])
                if step == "attn moments":
                    moments(dve, "attn", lane, e + 1)
                if step == "norm attn":
                    normalised(dve, "attn", lane, attn_n[lane][:, :], attn[:, e, :], e + 1, attn_normed)
                if step == "mid stats":
                    dve.wait_ge(mid_ready, e + 1)
                    stats("mid", lane, x_mid[lane][:, :])
                if step == "mid moments":
                    moments(dve, "mid", lane, e + 1)
                if step == "norm mid":
                    normalised(dve, "mid", lane, h_sb[lane][:, :], x_mid[lane][:, :], e + 1, h_ready)
                if step == "logits":
                    _, _, _, rstd = norm_of[f"mid{lane}"]
                    dve.wait_ge(rstd_of["mid"], e + 1)
                    dve.wait_ge(logits_ready, e + 1)
                    nc.vector.scalar_tensor_tensor(out=logit[lane][:, :], in0=aux_of_lane[lane][:, D:D + EXPERTS],
                                                   scalar=rstd[:, 0:1], in1=rb_sb[:, :], op0=ALU.mult,
                                                   op1=ALU.add).then_inc(logit_biased, 1)
                if step == "negate max":
                    dve.wait_ge(logit_biased, e + 1)
                    nc.vector.tensor_reduce(logit_nmax[lane][:, :], logit[lane][:, :], AX, ALU.max,
                                            negate=True).then_inc(logit_max_found, 1)
                if step == "top":
                    n = in_register(dve, e + 1)
                    dve.wait_ge(x_loaded[0], 16)
                    dve.wait_ge(logit_biased, n)
                    nc.vector.max(top[lane][:, :], logit[lane][:, :]).then_inc(top_found, 1)
                if step == "strike":
                    n = in_register(dve, e + 1)
                    dve.wait_ge(x_loaded[0], 16)
                    dve.wait_ge(top_found, n)
                    nc.vector.match_replace(struck[lane][:, :], top[lane][:, :], logit[lane][:, :],
                                            STRUCK).then_inc(top_struck, 1)
                if step == "choose":
                    dve.wait_ge(expo_ready, e + 1)
                    dve.wait_ge(top_struck, e + 1)
                    nc.vector.scalar_tensor_tensor(out=chosen[lane][:, 0:EXPERTS], in0=struck[lane][:, :],
                                                   scalar=STRUCK / 2, in1=expo[lane][:, :], op0=ALU.is_lt,
                                                   op1=ALU.mult).then_inc(chosen_ready, 1)
                if step == "sum top":
                    dve.wait_ge(chosen_ready, e + 1)
                    nc.vector.reduce_sum(top_sum[lane][:, :], chosen[lane][:, 0:EXPERTS],
                                         AX).then_inc(top_summed, 1)
                if step == "mix":
                    dve.wait_ge(mix_ready, e + 1)
                    dve.wait_ge(top_summed, e + 1)
                    nc.vector.scalar_tensor_tensor(out=y_sb[lane][:, :], in0=h_sb[lane][:, :],
                                                   scalar=top_sum[lane][:, 0:1], in1=aux_of_lane[lane][:, 0:D],
                                                   op0=ALU.mult, op1=ALU.add).then_inc(y_ready, 1)
                if step == "mix stats":
                    dve.wait_ge(y_ready, e + 1)
                    stats("mix", lane, y_sb[lane][:, :])
                if step == "mix moments":
                    moments(dve, "mix", lane, e + 1)
                if step == "centre attn":
                    dve.wait_ge(moments_of["attn"], e + 1)
                    nc.vector.tensor_scalar(attn_n[lane][:, :], attn[:, e, :], norm_of[f"attn{lane}"][1][:, 0:1],
                                            None, ALU.subtract).then_inc(attn_centred, 1)
                if step == "residual":
                    dve.wait_ge(attn_centred, lane)
                    dve.wait_ge(rstd_of["attn"], e + 1)
                    nc.vector.scalar_tensor_tensor(out=x_mid[lane][:, :], in0=attn_n[lane][:, :],
                                                   scalar=norm_of[f"attn{lane}"][3][:, 0:1], in1=x_sb[:, e, :],
                                                   op0=ALU.mult, op1=ALU.add).then_inc(mid_ready, 1)
                if step == "centre mix":
                    dve.wait_ge(moments_of["mix"], e + 1)
                    nc.vector.tensor_scalar(y_n[lane][:, :], y_sb[lane][:, :], norm_of[f"mix{lane}"][1][:, 0:1],
                                            None, ALU.subtract).then_inc(y_centred, 1)
                if step == "output":
                    dve.wait_ge(y_centred, lane)
                    dve.wait_ge(rstd_of["mix"], e + 1)
                    nc.vector.scalar_tensor_tensor(out=out_sb[:, e, :], in0=y_n[lane][:, :],
                                                   scalar=norm_of[f"mix{lane}"][3][:, 0:1], in1=x_mid[lane][:, :],
                                                   op0=ALU.mult, op1=ALU.add).then_inc(out_ready, 1)

            def centre_router():
                dve.wait_ge(small_loaded, 16 * 3)
                dve.wait_ge(router_averaged, 1)
                for c in range(KD):
                    nc.vector.tensor_tensor(rw_mid[:, c, :], rw_sb[:, c, :], aux_ps[0][:, D:D + EXPERTS],
                                            ALU.subtract).then_inc(router_centred, 1)

            def v_low(G, slot):
                dve.wait_ge(v_hi_done, G + 1)
                nc.vector.scalar_tensor_tensor(out=v_lo[:, slot, :, :, :].rearrange("p m h n -> p (m h n)"),
                                               in0=v_ps[slot][:, :], scalar=QKV_DOWN,
                                               in1=v_hi[:, slot, :, :, :].rearrange("p m h n -> p (m h n)"),
                                               op0=ALU.mult, op1=ALU.subtract).then_inc(v_split, 1)

            STEPS = {1: ("attn stats", "attn moments"), 3: ("norm mid",), 5: ("logits", "negate max"),
                     6: ("choose", "sum top"), 7: ("mix",)}
            STEPS_AT_END = {1: ("norm attn",), 2: ("mid stats", "mid moments"), 5: ("top", "strike"),
                            7: ("mix stats", "mix moments")}
            LAST_STEPS = {1: ("attn stats", "attn moments"), 3: ("norm mid",), 5: ("logits", "negate max")}
            LAST_STEPS_AT_END = {1: ("norm attn",), 2: ("mid stats", "mid moments"), 5: ("top", "strike"),
                                 6: ("choose", "sum top")}

            def negate_scores(t, k):
                U = number(t, k)
                if exists(t, k, 1):
                    s = (k + 1) % 2
                    n = in_register(dve, U + 2)
                    dve.wait_ge(consts_ready, 3)
                    dve.wait_ge(scores_ready, n)
                    nc.vector.tensor_tensor_reduce(neg_scores[:, s, 0:P], s_ps[:, 0:P], mask[:, P:2 * P], -S_SCALE,
                                                   HUGE, ALU.add, ALU.min, neg_max[:, s, 0:1])
                    nc.vector.tensor_tensor_reduce(neg_scores[:, s, P:3 * P], s_ps[:, P:3 * P], mask[:, :], -S_SCALE,
                                                   HUGE, ALU.add, ALU.min,
                                                   neg_max[:, s, 1:2]).then_inc(neg_max_ready, 1)

            def values_low(t, k):
                if k % 2 == 0 and exists(t, k, 0):
                    v_low(pair_number(t, k), k // 2 % 2)

            def later_weights_low(t, k):
                U = number(t, k)
                if is_int(t) and EARLY <= U + 4 < HEADS:
                    weights_low(U + 4, 0, VW, w_hi_by_pool, U + 1, qk_weights_split)

            def probs_low(t, k):
                U = number(t, k)
                if exists(t, k, 0):
                    dve.wait_ge(pT_hi_done, U + 1)
                    nc.vector.scalar_tensor_tensor(out=pT_lo[:, k % 2, :], in0=pT_ps[:, 0:3 * P], scalar=1.0,
                                                   in1=pT_hi[:, k % 2, :], op0=ALU.mult,
                                                   op1=ALU.subtract).then_inc(pT_split, 1)

            def queries_keys_low(t, k):
                U = number(t, k)
                if exists(t, k, 2):
                    dve.wait_ge(qk_hi_done, U + 3)
                    nc.vector.scalar_tensor_tensor(out=qk_lo[:, k % 2, :], in0=qk_bank(t, k)[:, :], scalar=QKV_DOWN,
                                                   in1=qk_hi[:, k % 2, :], op0=ALU.mult,
                                                   op1=ALU.subtract).then_inc(qk_split, 1)

            def invert_sums(t, k):
                U = number(t, k)
                if exists(t, k, 1):
                    s = (k + 1) % 2
                    dve.wait_ge(probs_exped, U + 2)
                    nc.vector.reciprocal(inv_sum[:, s, :], row_sum[:, s, :]).then_inc(sums_inverted, 1)
                    if is_int(t) and U + 1 == UNITS - 1:
                        dve.wait_ge(sums_inverted, U + 2)
                        nc.vector.tensor_scalar(probs[:, s, 0:P], probs[:, s, 0:P], inv_sum[:, s, 0:1], P_SCALE,
                                                ALU.mult, ALU.mult)
                        nc.vector.tensor_scalar(probs[:, s, P:3 * P], probs[:, s, P:3 * P], inv_sum[:, s, 1:2],
                                                P_SCALE, ALU.mult, ALU.mult).then_inc(probs_scaled, 1)

            def fill():
                queries_keys_low(-1, 6)
                weights_low(2, 0, VW, w_hi_by_act, 5, qk_weights_split)
                negate_scores(-1, 7)
                queries_keys_low(-1, 7)
                weights_low(2, VW, WCOLS, w_hi_by_act, 6, vo_weights_split)
                invert_sums(-1, 7)
                negate_scores(0, 0)
                values_low(0, 0)
                weights_low(3, VW, WCOLS, w_hi_by_act, 8, vo_weights_split)
                invert_sums(0, 0)
                probs_low(0, 0)
                queries_keys_low(0, 0)
                weights_low(3, 0, VW, w_hi_by_act, 7, qk_weights_split)
                later_weights_low(0, 0)

            def unit(t, k):
                U = number(t, k)
                in_finish = not is_int(t) or 2 <= t <= LAST
                negate_scores(t, k)
                if exists(t, k, -1):
                    dve.wait_ge(z_hi_done, U)
                    nc.vector.scalar_tensor_tensor(out=z_lo[:, (k + 1) % 2, :], in0=z_ps[:, 0:SEQ], scalar=Z_DOWN,
                                                   in1=z_hi[:, (k + 1) % 2, :], op0=ALU.mult,
                                                   op1=ALU.subtract).then_inc(z_split, 1)
                probs_low(t, k)
                if is_int(t) and U - 2 in X_TILE_AT:
                    token_normalise(X_TILE_AT[U - 2])
                values_low(t, k)
                if in_finish:
                    for step in (LAST_STEPS if is_last(t) else STEPS).get(k, ()):
                        finish(0, t - 2, step)
                invert_sums(t, k)
                queries_keys_low(t, k)
                later_weights_low(t, k)
                if is_int(t):
                    if U - 3 in X_TILE_AT:
                        tokens_low(X_TILE_AT[U - 3])
                    if U in X_TILE_AT:
                        token_moments(X_TILE_AT[U])
                if is_int(t) and U == HEADS - 1:
                    centre_router()
                if k == 7 and is_last(t):
                    add_attention(t + 1)
                if k == 0 and not (is_int(t) and (t < 1 or t > LAST)):
                    if is_int(t) and t == 1:
                        dve.wait_ge(attn_cleared, 1 + len(lanes))
                    add_attention(t)
                if in_finish:
                    for step in (LAST_STEPS_AT_END if is_last(t) else STEPS_AT_END).get(k, ()):
                        finish(0, t - 2, step)

            token_moments(0)
            token_moments(1)
            token_normalise(0)
            token_normalise(1)
            weights_low(0, 0, VW, w_hi_by_act, 1, qk_weights_split)
            tokens_low(0)
            tokens_low(1)
            weights_low(1, 0, VW, w_hi_by_act, 2, qk_weights_split)
            weights_low(0, VW, WCOLS, w_hi_by_act, 3, vo_weights_split)
            weights_low(1, VW, WCOLS, w_hi_by_act, 4, vo_weights_split)
            all_units(dve, fill, unit)
            for lane, step in ((1, "last head"), (1, "attn stats"), (2, "last head"), (1, "attn moments"),
                               (2, "attn stats"), (1, "centre attn"), (2, "attn moments"), (2, "centre attn"),
                               (1, "residual"), (1, "mid stats"), (2, "residual"), (1, "mid moments"),
                               (2, "mid stats"), (2, "mid moments"), (0, "mix"), (0, "mix stats"), (1, "logits"),
                               (1, "negate max"), (2, "logits"), (1, "top"), (2, "negate max"), (2, "top"),
                               (1, "strike"), (1, "choose"), (2, "strike"), (0, "mix moments"), (2, "choose"),
                               (1, "norm mid"), (1, "sum top"), (2, "norm mid"), (2, "sum top"), (1, "mix"),
                               (1, "mix stats"), (2, "mix"), (1, "mix moments"), (2, "mix stats"),
                               (1, "centre mix"), (2, "mix moments"), (2, "centre mix"), (1, "output"),
                               (2, "output")):
                finish(lane, TILES - 3 + lane, step)

        @block.tensor
        def _(pe):
            SPLIT = ((0, 0), (0, 1), (1, 0))
            SPLIT_CHUNKS = [(0, j, c) for c in range(KD) for j in (0, 1)] + [(1, 0, c) for c in range(KD)]
            w = (w_hi, w_lo)
            xT = (xT_hi, xT_lo)
            qk = (qk_hi, qk_lo)
            v = (v_hi, v_lo)
            pT = (pT_hi, pT_lo)
            z = (z_hi, z_lo)

            def place(t, k, ahead, half, batch, next_half, next_batch):
                if is_int(t):
                    return (ITER * t + k + ahead) % HEADS, (ITER * t + k + ahead) // HEADS
                if k + ahead < 0:
                    return next_half * ITER + (k + ahead + ITER), None
                if k + ahead < ITER:
                    return half * ITER + (k + ahead), batch
                return next_half * ITER + (k + ahead - ITER), next_batch

            def tokens_turn(i):
                pe.wait_ge(x_normed, i + 1)
                for c in range(KD):
                    last = nc.tensor.transpose(aux_ps[i == 1][:, c * P:(c + 1) * P], xn[:, i % 2, c * P:(c + 1) * P],
                                               ident[:, :])
                last.then_inc(x_turned, 1)

            def finish(lane, e, step):
                if step == "turn mid":
                    pe.wait_ge(mid_ready, e + 1)
                    for c in range(KD):
                        last = nc.tensor.transpose(aux_of_lane[lane][:, c * P:(c + 1) * P],
                                                   x_mid[lane][:, c * P:(c + 1) * P], ident[:, :])
                    last.then_inc(mid_turned, 1)
                if step == "route":
                    pe.wait_ge(midT_ready, e + 1)
                    for c in range(KD):
                        last = nc.tensor.matmul(aux_of_lane[lane][:, D:D + EXPERTS], midT[lane][:, c, :],
                                                rw_mid[:, c, :],
                                                start=(c == 0), stop=(c == KD - 1))
                    last.then_inc(logits_ready, 1)
                if step == "turn chosen":
                    pe.wait_ge(chosen_ready, e + 1)
                    nc.tensor.transpose(aux_of_lane[lane][:, 320:320 + P], chosen[lane][:, :],
                                        ident[:, :]).then_inc(chosen_turned, 1)
                if step == "mix":
                    pe.wait_ge(chosenT_ready, e + 1)
                    nc.tensor.matmul(aux_of_lane[lane][:, 0:D], chosenT[lane][0:EXPERTS, :], eb_sb[:, :],
                                     start=True, stop=True).then_inc(mix_ready, 1)

            STEPS = {3: ("turn mid",), 4: ("route",), 6: ("turn chosen",)}
            LAST_STEPS = {3: ("turn mid",), 4: ("route",)}

            def where(t):
                return (None,) * 4 if is_int(t) else regs

            def scores(t, k):
                U = number(t, k)
                if exists(t, k, 1):
                    pe.wait_ge(qk_split, U + 2)
                    if positive(U + 1):
                        pe.wait_ge(neg_max_ready, U + 1)
                    s = (k + 1) % 2
                    for n, (i, j) in enumerate(SPLIT):
                        nc.tensor.matmul(s_ps[:, 0:P], qk[i][:, s, 0:P], qk[j][:, s, SEQ:SEQ + P],
                                         start=(n == 0), stop=(n == 2))
                    for n, (i, j) in enumerate(SPLIT):
                        last = nc.tensor.matmul(s_ps[:, P:3 * P], qk[i][:, s, P:2 * P], qk[j][:, s, SEQ:2 * SEQ],
                                                start=(n == 0), stop=(n == 2))
                    last.then_inc(scores_ready, 1)

            def turn_probs(t, k):
                U = number(t, k)
                if exists(t, k, 0):
                    pe.wait_ge(probs_scaled, U + 1)
                    if positive(U):
                        pe.wait_ge(pT_split, U)
                    for n in range(3):
                        last = nc.tensor.transpose(pT_ps[:, n * P:(n + 1) * P], probs[:, k % 2, n * P:(n + 1) * P],
                                                   ident[:, :])
                    last.then_inc(probs_turned, 1)

            def project_qk(t, k):
                U = number(t, k)
                if exists(t, k, 2):
                    h, b = place(t, k, 2, *where(t))
                    if is_int(t):
                        pe.wait_ge(qk_weights_split, min(U + 3, HEADS))
                        pe.wait_ge(x_split, 2 * (b + 1))
                    cols = bass.ds(b * SEQ, SEQ)
                    for part, base in ((0, QW), (1, KW)):
                        for n, (i, j, c) in enumerate(SPLIT_CHUNKS):
                            last = nc.tensor.matmul(qk_bank(t, k)[:, part * SEQ:(part + 1) * SEQ],
                                                    w[i][:, h, base + c * P:base + (c + 1) * P],
                                                    xT[j][:, c, cols], start=(n == 0), stop=(n == 5))
                    last.then_inc(qk_projected, 1)

            def project_v(t, k):
                U = number(t, k)
                if exists(t, k, 2 - k % 2):
                    h, b = place(t, k, 2 - k % 2, *where(t))
                    a = k % 2
                    if a == 0 and positive(pair_number(t, k)):
                        pe.wait_ge(v_split, pair_number(t, k))
                    if is_int(t) and U + 2 < HEADS:
                        if h + 1 < EARLY:
                            pe.wait_ge(vo_weights_split, h + 2)
                        else:
                            pe.wait_ge(vo_weights_low, h + 2 - EARLY)
                    for n, (i, j, c) in enumerate(SPLIT_CHUNKS):
                        last = nc.tensor.matmul(v_ps[(k // 2 + 1) % 2][:, a * 2 * DH:(a + 1) * 2 * DH],
                                                xT[i][:, c, bass.ds(b * SEQ + a * P, P)],
                                                w[j][:, bass.ds(h, 2), VW + c * P:VW + (c + 1) * P],
                                                start=(n == 0), stop=(n == 5))
                    if a == 1:
                        last.then_inc(v_projected, 1)

            def values(t, k):
                U = number(t, k)
                if exists(t, k, 0):
                    pe.wait_ge(pT_split, U + 1)
                    pe.wait_ge(v_split, pair_number(t, k) + 1)
                    g, hh, s = k // 2 % 2, k % 2, k % 2
                    for n, (i, j) in enumerate(SPLIT):
                        nc.tensor.matmul(z_ps[:, 0:SEQ], v[i][:, g, 0, hh, :], pT[j][:, s, 0:SEQ],
                                         start=(n == 0), stop=False, skip_group_check=True)
                    for n, (i, j) in enumerate(SPLIT):
                        last = nc.tensor.matmul(z_ps[:, P:SEQ], v[i][:, g, 1, hh, :], pT[j][:, s, SEQ:3 * P],
                                                start=False, stop=(n == 2), skip_group_check=True)
                    last.then_inc(z_summed, 1)

            def fill():
                project_qk(-1, 6)
                project_qk(-1, 7)
                scores(-1, 7)
                project_v(-1, 6)
                project_v(-1, 7)
                scores(0, 0)
                project_qk(0, 0)
                turn_probs(0, 0)
                project_v(0, 0)
                values(0, 0)

            def unit(t, k):
                U = number(t, k)
                scores(t, k)
                turn_probs(t, k)
                if not is_int(t) or 2 <= t <= LAST:
                    if k == 7:
                        finish(0, t - 2, "turn chosen" if is_last(t) else "mix")
                project_qk(t, k)
                if exists(t, k, -1):
                    pe.wait_ge(z_split, U)
                    if k == 1 and positive(t):
                        pe.wait_ge(attn_added, t)
                    ends = is_int(t) and t > LAST
                    if ends:
                        pe.wait_ge(attn_added, t)
                    h, _ = place(t, k, -1, *where(t))
                    s = (k + 1) % 2
                    for a in range(2):
                        for n, (i, j) in enumerate(SPLIT):
                            dst = last_o[a][:, 0:D] if ends else o_ps[:, a * D:(a + 1) * D]
                            last = nc.tensor.matmul(dst, z[i][:, s, a * P:(a + 1) * P], w[j][:, h, OW:OW + D],
                                                    start=(n == 0 and (ends or (k == 1 and a == 0))),
                                                    stop=(k == 0 or (k == 7 and is_last(t))), skip_group_check=True)
                        if ends:
                            last.then_inc(o_summed, 1)
                    if (k == 0 and not ends) or (k == 7 and is_last(t)):
                        last.then_inc(o_summed, 1)
                project_v(t, k)
                if is_int(t) and U - 2 in X_TILE_AT:
                    tokens_turn(X_TILE_AT[U - 2])
                if is_int(t) and U == HEADS - 1:
                    pe.wait_ge(x_split, TILES)
                    pe.wait_ge(consts_ready, 4)
                    pe.wait_ge(small_loaded, 16 * 3)
                    for c in range(KD):
                        last = nc.tensor.matmul(aux_ps[0][:, D:D + EXPERTS], averager[:, :], rw_sb[:, c, :],
                                                start=(c == 0), stop=(c == KD - 1))
                    last.then_inc(router_averaged, 1)
                if not is_int(t) or 2 <= t <= LAST:
                    for step in (LAST_STEPS if is_last(t) else STEPS).get(k, ()):
                        finish(0, t - 2, step)
                values(t, k)
                if k == 7 and is_last(t):
                    finish(0, t - 2, "mix")

            def keep_busy(count):
                for n in range(count):
                    nc.tensor.transpose(z_ps[:, 0:P], ident[:, :], ident[:, :])

            pe.wait_ge(consts_ready, 2)
            keep_busy(17)
            tokens_turn(0)
            keep_busy(1)
            tokens_turn(1)
            keep_busy(6)
            regs = None
            fill()
            for U in range(1, 2 * ITER):
                unit(U // ITER, U % ITER)
            with pe.Fori(2, LAST) as t:
                regs = (pe.snap(t % 2), pe.snap(t // 2), pe.snap((t + 1) % 2), pe.snap((t + 1) // 2))
                for k in range(ITER):
                    unit(t, k)
            for k in range(ITER):
                unit(LAST, k)
            unit(LAST + 1, 0)
            keep_busy(24)
            for lane in (1, 2):
                finish(lane, TILES - 3 + lane, "turn mid")
                keep_busy(4)
            for lane in (1, 2):
                finish(lane, TILES - 3 + lane, "route")
            for lane in (1, 2):
                finish(lane, TILES - 3 + lane, "turn chosen")
            for lane in (1, 2):
                finish(lane, TILES - 3 + lane, "mix")


def kernel(**inputs):
    import numpy as _np
    import concourse.bacc as _bacc
    from concourse.bass_utils import run_bass_kernel_spmd as _run

    x = _np.ascontiguousarray(inputs["L0_attn_x"]).reshape(B * SEQ, D)

    def head_rows(w):
        w = _np.asarray(w).transpose(0, 2, 1).reshape(HEADS, KD, P, DH)
        return w.transpose(0, 2, 1, 3).reshape(HEADS, P, KD * DH)

    w_o = _np.asarray(inputs["L0_attn_W_O"]).transpose(0, 2, 1)
    weights = _np.ascontiguousarray(_np.concatenate(
        [head_rows(inputs["L0_attn_W_Q"]), head_rows(inputs["L0_attn_W_K"]), head_rows(inputs["L0_attn_W_V"]), w_o],
        axis=2))
    router_w = _np.ascontiguousarray(
        _np.asarray(inputs["L0_ffn_router_weight"]).T.reshape(KD, P, EXPERTS).transpose(1, 0, 2))
    router_b = _np.ascontiguousarray(_np.broadcast_to(_np.asarray(inputs["L0_ffn_router_bias"]), (P, EXPERTS)))
    expert_b = _np.ascontiguousarray(inputs["L0_ffn_expert_bias"])

    nc = _bacc.Bacc("TRN2", target_bir_lowering=False, num_devices=1)
    arrays, args = {}, []
    for name, a in (("x", x), ("weights", weights), ("router_w", router_w), ("router_b", router_b),
                    ("expert_b", expert_b)):
        arrays[f"in_{name}_dram"] = a
        args.append(nc.dram_tensor(f"in_{name}_dram", a.shape, F32, kind="ExternalInput").ap())
    args.append(nc.dram_tensor("out_0_dram", (B * SEQ, D), F32, kind="ExternalOutput").ap())
    layer_kernel(nc, *args)
    r = _run(nc, [arrays], core_ids=[0])
    return r.results[0]["out_0_dram"].reshape(B, SEQ, D)
```
